# Optimizing a Trainium2 kernel written in Bass

```python
import numpy as np
import jax
import jax.numpy as jnp

def _softmax(x, axis=-1):
    return jax.nn.softmax(x, axis=axis)

def _gelu(x):
    return jax.nn.gelu(x, approximate=True)

def _silu(x):
    return jax.nn.silu(x)

def _sigmoid(x):
    return jax.nn.sigmoid(x)

def _layernorm(x, axis=-1, eps=1e-05):
    m = jnp.mean(x, axis=axis, keepdims=True)
    v = jnp.var(x, axis=axis, keepdims=True)
    return (x - m) / jnp.sqrt(v + eps)

def _scatter_add(tgt, idx, src, axis=0):
    return tgt.at[idx].add(src)

def _segment_sum(src, seg, n):
    return jax.ops.segment_sum(src, seg, n)
kernel_name = 'mk_adaln_ffn_d1_seqx_r4_58c795'

def setup_inputs(seed: int=0):
    np.random.seed(seed)
    _w = jnp.asarray

    def _rec_inputs():
        import jax
        import jax.numpy as jnp
        _rk = jax.random.key(seed)
        x = -7.109e-05 + 0.9999 * jax.random.normal(jax.random.fold_in(_rk, 1), (16, 256, 512), jnp.float32)
        _lenS = 256 - jax.random.randint(jax.random.fold_in(_rk, 7), (16,), 0, max(1, 256 // 4) + 1, jnp.int32)
        _lenS2 = 256 - jax.random.randint(jax.random.fold_in(_rk, 8), (16,), 0, max(1, 256 // 4) + 1, jnp.int32)
        itok_B_0_6 = jax.random.randint(jax.random.fold_in(_rk, 11), (16,), 0, 7, jnp.int32)
        return (x, itok_B_0_6)
    x, itok_B_0_6 = _rec_inputs()

    def _L0_cond_setup():
        import jax, jax.numpy as jnp
        import numpy as np
        B, T, D_IN, D_OUT = (16, 512, 512, 512)
        N_ADAPTERS, RANK = (8, 16)
        key = jax.random.key(seed)
        k_x, k_w, k_a, k_b, k_s, k_idx = jax.random.split(key, 6)
        x = jax.random.normal(k_x, (B, T, D_IN), dtype=jnp.float32)
        W = jax.random.normal(k_w, (D_OUT, D_IN), dtype=jnp.float32) * (1.0 / np.sqrt(D_IN))
        A = jax.random.normal(k_a, (N_ADAPTERS, RANK, D_IN), dtype=jnp.float32) * 0.02
        Bm = jax.random.normal(k_b, (N_ADAPTERS, D_OUT, RANK), dtype=jnp.float32) * 0.02
        scalings = jnp.ones((N_ADAPTERS,), dtype=jnp.float32)
        adapter_idx = jax.random.randint(k_idx, (B,), 0, N_ADAPTERS, dtype=jnp.int32)
        return {'x': x, 'W': W, 'A': A, 'Bm': Bm, 'scalings': scalings, 'adapter_idx': adapter_idx}
    _L0_cond_all = _L0_cond_setup()
    _L0_cond_in = {k: v for k, v in _L0_cond_all.items() if k in ('W', 'A', 'Bm', 'scalings')}
    del _L0_cond_all

    def _L0_ffn_setup():
        import jax, jax.numpy as jnp
        import numpy as np
        TOP_K = 6
        CAP_FACTOR = 2

        def _shared_swiglu(x, wg, wu, wd):
            return jax.nn.silu(x @ wg.T) * (x @ wu.T) @ wd.T
        key = jax.random.key(seed)
        ks = jax.random.split(key, 8)
        B, S, D, E, F, FS = (4, 512, 512, 64, 352, 704)
        scale = jnp.float32(0.02)
        return {'hidden_states': jax.random.normal(ks[0], (B, S, D), jnp.float32), 'gate_w': jax.random.normal(ks[1], (E, D), jnp.float32) * scale, 'w_gate': jax.random.normal(ks[2], (E, F, D), jnp.float32) * scale, 'w_up': jax.random.normal(ks[3], (E, F, D), jnp.float32) * scale, 'w_down': jax.random.normal(ks[4], (E, D, F), jnp.float32) * scale, 'sh_gate': jax.random.normal(ks[5], (FS, D), jnp.float32) * scale, 'sh_up': jax.random.normal(ks[6], (FS, D), jnp.float32) * scale, 'sh_down': jax.random.normal(ks[7], (D, FS), jnp.float32) * scale}
    _L0_ffn_all = _L0_ffn_setup()
    _L0_ffn_in = {k: v for k, v in _L0_ffn_all.items() if k in ('gate_w', 'w_gate', 'w_up', 'w_down', 'sh_gate', 'sh_up', 'sh_down')}
    del _L0_ffn_all
    return {'x': x, 'itok_B_0_6': itok_B_0_6, 'L0_cond_W': _L0_cond_in['W'], 'L0_cond_A': _L0_cond_in['A'], 'L0_cond_Bm': _L0_cond_in['Bm'], 'L0_cond_scalings': _L0_cond_in['scalings'], 'L0_ffn_gate_w': _L0_ffn_in['gate_w'], 'L0_ffn_w_gate': _L0_ffn_in['w_gate'], 'L0_ffn_w_up': _L0_ffn_in['w_up'], 'L0_ffn_w_down': _L0_ffn_in['w_down'], 'L0_ffn_sh_gate': _L0_ffn_in['sh_gate'], 'L0_ffn_sh_up': _L0_ffn_in['sh_up'], 'L0_ffn_sh_down': _L0_ffn_in['sh_down']}

def reference(x, itok_B_0_6, L0_cond_W, L0_cond_A, L0_cond_Bm, L0_cond_scalings, L0_ffn_gate_w, L0_ffn_w_gate, L0_ffn_w_up, L0_ffn_w_down, L0_ffn_sh_gate, L0_ffn_sh_up, L0_ffn_sh_down):
    import jax
    import jax.numpy as jnp

    def _L0_cond_ref(x, W, A, Bm, scalings, adapter_idx):
        import jax, jax.numpy as jnp
        import numpy as np
        B, T, D_IN, D_OUT = (16, 512, 512, 512)
        N_ADAPTERS, RANK = (8, 16)
        H = jnp.einsum('btd,od->bto', x, W)
        A_b = A[adapter_idx]
        B_b = Bm[adapter_idx]
        s_b = scalings[adapter_idx]
        xa = jnp.einsum('btd,brd->btr', x, A_b)
        delta = jnp.einsum('btr,bor->bto', xa, B_b)
        delta = jax.lax.stop_gradient(delta * s_b[:, None, None])
        return H + delta

    def _L0_ffn_ref(hidden_states, gate_w, w_gate, w_up, w_down, sh_gate, sh_up, sh_down):
        import jax, jax.numpy as jnp
        import numpy as np
        TOP_K = 6
        CAP_FACTOR = 2

        def _shared_swiglu(x, wg, wu, wd):
            return jax.nn.silu(x @ wg.T) * (x @ wu.T) @ wd.T
        B, S, D = hidden_states.shape
        E = gate_w.shape[0]
        x = hidden_states.reshape(-1, D)
        N = x.shape[0]
        A = N * TOP_K
        C = CAP_FACTOR * ((A + E - 1) // E)
        scores = jax.nn.softmax(x @ gate_w.T, axis=-1)
        topk_w, topk_idx = jax.lax.top_k(scores, TOP_K)
        topk_w = topk_w / (topk_w.sum(-1, keepdims=True) + 1e-20)
        flat_e = topk_idx.reshape(-1)
        flat_w = topk_w.reshape(-1)
        order = jnp.argsort(flat_e)
        se = flat_e[order]
        st = order // TOP_K
        sw = flat_w[order]
        counts = jnp.bincount(flat_e, length=E)
        offsets = jnp.cumsum(counts) - counts
        pos = jnp.arange(A) - offsets[se]
        valid = pos < C
        pos_c = jnp.minimum(pos, C - 1)
        buf = jnp.zeros((E, C, D), x.dtype).at[se, pos_c].add(jnp.where(valid[:, None], x[st], jnp.zeros((), x.dtype)))
        g = jnp.einsum('ecd,efd->ecf', buf, w_gate)
        u = jnp.einsum('ecd,efd->ecf', buf, w_up)
        eo = jnp.einsum('ecf,edf->ecd', jax.nn.silu(g) * u, w_down)
        gathered = eo[se, pos_c] * (sw * valid.astype(sw.dtype))[:, None]
        y = jnp.zeros_like(x).at[st].add(gathered).reshape(B, S, D)
        return y + _shared_swiglu(hidden_states, sh_gate, sh_up, sh_down)
    x = x + _L0_ffn_ref(_L0_cond_ref(x, L0_cond_W, L0_cond_A, L0_cond_Bm, L0_cond_scalings, itok_B_0_6), L0_ffn_gate_w, L0_ffn_w_gate, L0_ffn_w_up, L0_ffn_w_down, L0_ffn_sh_gate, L0_ffn_sh_up, L0_ffn_sh_down)
    return x

_drawn_inputs = setup_inputs


def setup_inputs(seed=0):
    import zlib

    import numpy as np

    out = dict(_drawn_inputs(seed))
    spreads = {'L0_cond_scalings': (1.0, 0.6)}
    factors = {'L0_cond_A': 8.0,
     'L0_cond_Bm': 8.0,
     'L0_ffn_gate_w': 2.905,
     'L0_ffn_w_gate': 2.85,
     'L0_ffn_w_up': 2.772,
     'L0_ffn_w_down': 2.775}
    for name, (base, spread) in spreads.items():
        noise = np.random.default_rng([zlib.crc32(name.encode()), seed]).standard_normal(out[name].shape)
        drawn = base * np.exp(spread * noise) if base else spread * noise
        out[name] = jnp.asarray(drawn.astype(out[name].dtype))
    for name, factor in factors.items():
        out[name] = (out[name] * factor).astype(out[name].dtype)
    return out
```

```python
import concourse.bass as bass
from concourse import mybir
from contextlib import ExitStack

P = 128
TOK, D = 4096, 512
BATCH, SEQ = 16, 256
KD = D // P
E, TOPK = 64, 6
F = 352
FC = [(0, 128), (128, 128), (256, 96)]
FS = 704
FSC = [(c * P, min(P, FS - c * P)) for c in range(6)]
CAP = 2 * ((TOK * TOPK + E - 1) // E)
CT = CAP // P
NCOL = 512
WROW = KD * 2 * F + 3 * D
NCH = 8
CH = WROW // NCH
NLD = 4
LD = WROW // NLD
GU0, DN0 = 0, KD * 2 * F
GRP = 512
NG = TOK // GRP
DROP = 1048576.0

C_ID, C_TRI, C_ONE, C_IOTA, C_G, C_TG, C_M, C_AD, C_P = 0, 128, 256, 384, 448, 960, 964, 972, 973
C_E = 974
NCONST = 975

T_WORD, T_COL = range(2)
NF = 2


def moe_kernel(nc, xT, xn, WT, AT, BT, scal, idx, gwT, cst, pad, shg, shd0, shd1, wE, out):
    f32, f32r, bf16, i32, u32 = (mybir.dt.float32, mybir.dt.float32r, mybir.dt.bfloat16,
                                 mybir.dt.int32, mybir.dt.uint32)
    ALU, ACT, AX = mybir.AluOpType, mybir.ActivationFunctionType, mybir.AxisListType

    H_d = nc.dram_tensor("H_rows", (TOK + P, D), f32).ap()
    HT_d = nc.dram_tensor("H_cols", (NG, P, KD, GRP), f32).ap()
    slot_d = nc.dram_tensor("slot_token", (NCOL * P, 2), f32).ap()
    tab_d = nc.dram_tensor("tile_table", (NCOL, NF), i32).ap()
    y_d = nc.dram_tensor("expert_sum", (TOK + P, D), f32).ap()

    top = ExitStack()
    with top:
        def sb(ctx, name, shape, dt=f32):
            return ctx.enter_context(nc.sbuf_tensor(name, shape, dt))

        def ps(ctx, name, shape=(P, 512), dt=f32):
            return ctx.enter_context(nc.psum_tensor(name, list(shape), dt))

        def sem(name):
            return top.enter_context(nc.semaphore(name))

        waits_passed = {n: sem(f"waits_passed_{n}") for n in ("sp", "act", "dve", "pool")}

        def hold(eng, name):
            eng.sem_inc(waits_passed[name], 1)

        class Steps:

            def __init__(self, eng, name):
                self.eng, self.sem, self.n = eng, sem(name), 0

            def next(self, ins, base=0):
                self.n += 1
                ins.then_inc(self.sem, 1)
                self.eng.wait_ge(self.sem, base + self.n)

        shgh = sb(top, "shgh", [P, KD, 2 * FS], f32r)
        shgl = sb(top, "shgl", [P, KD, 2 * FS], f32r)
        shdh = sb(top, "shdh", [P, 6, D], f32r)
        shdl = sb(top, "shdl", [P, 6, D], f32r)
        ident = sb(top, "ident", [P, P])
        idxT = sb(top, "idxT", [P, NCOL], i32)
        wT = sb(top, "wT", [P, NCOL])
        tab = sb(top, "tab", [1, NCOL * NF], i32)
        bnd = sb(top, "bnd", [1, E], i32)
        tot = sb(top, "tot", [1, 2], i32)

        def split_mm(out_, lh, ll, rh, rl, first, last):
            nc.tensor.matmul(out_, lh, rh, start=first, stop=False)
            nc.tensor.matmul(out_, lh, rl, start=False, stop=False)
            return nc.tensor.matmul(out_, ll, rh, start=False, stop=last)

        with ExitStack() as ctx:
            c = sb(ctx, "cst", [P, NCONST])
            wt_raw = sb(ctx, "wt_raw", [P, KD, D])
            at_raw = sb(ctx, "at_raw", [P, KD, P])
            bt_raw = sb(ctx, "bt_raw", [P, D])
            gw = sb(ctx, "gw", [P, KD, E])
            scl = sb(ctx, "scl", [P, 1])
            idb = sb(ctx, "idb", [P, BATCH], i32)
            sh_raw = sb(ctx, "sh_raw", [P, 2, 2 * FS])
            wth, wtl = sb(ctx, "wth", [P, KD, D], f32r), sb(ctx, "wtl", [P, KD, D], f32r)
            ath, atl = sb(ctx, "ath", [P, KD, P], f32r), sb(ctx, "atl", [P, KD, P], f32r)
            bth, btl = sb(ctx, "bth", [P, D], f32r), sb(ctx, "btl", [P, D], f32r)
            idf = sb(ctx, "idf", [P, BATCH])
            amask = sb(ctx, "amask", [P, BATCH])
            tri = sb(ctx, "tri", [P, P], bf16)
            one = sb(ctx, "one", [P, P], bf16)
            zero = sb(ctx, "zero", [P, NCOL])
            xraw = [sb(ctx, f"xraw{p}", [P, KD, SEQ]) for p in range(2)]
            xh = [sb(ctx, f"xh{p}", [P, KD, SEQ], f32r) for p in range(2)]
            xl = [sb(ctx, f"xl{p}", [P, KD, SEQ], f32r) for p in range(2)]
            xam = sb(ctx, "xam", [P, SEQ])
            xah, xal = sb(ctx, "xah", [P, SEQ], f32r), sb(ctx, "xal", [P, SEQ], f32r)
            H_s = sb(ctx, "H_s", [P, 2, D])
            HT_s = sb(ctx, "HT_s", [P, KD, SEQ])
            nm = sb(ctx, "nm", [P, 2])
            ex = sb(ctx, "ex", [P, 2, E])
            S = sb(ctx, "S", [P, 2])
            rS = sb(ctx, "rS", [P, 2])
            sc = sb(ctx, "sc", [P, 2, E])
            top8 = sb(ctx, "top8", [P, 2, 8])
            ix8 = sb(ctx, "ix8", [P, 2, 8], u32)
            ixf = sb(ctx, "ixf", [P, 2, TOPK])
            ssum = sb(ctx, "ssum", [P, 2])
            rsum = sb(ctx, "rsum", [P, 2])
            base6 = [sb(ctx, f"base6{p}", [P, 2, TOPK]) for p in range(2)]
            w6 = [sb(ctx, f"w6{p}", [P, 2, TOPK]) for p in range(2)]
            hot = [sb(ctx, f"hot{p}", [P, 2, TOPK, E]) for p in range(2)]
            prod = sb(ctx, "prod", [P, 2, TOPK, E])
            M = [sb(ctx, f"M{p}", [P, 2, E], bf16) for p in range(2)]
            acc = [sb(ctx, f"acc{p}", [P, 2, E], bf16) for p in range(2)]
            pos6 = sb(ctx, "pos6", [P, 2, TOPK])
            dst6 = sb(ctx, "dst6", [P, 2, TOPK])
            over = sb(ctx, "over", [P, 2, TOPK])
            sc6 = sb(ctx, "sc6", [P, 2, TOPK])
            scI = [sb(ctx, f"scI{p}", [P, 2 * TOPK], i32) for p in range(2)]
            tokf = [sb(ctx, f"tokf{p}", [P, 2]) for p in range(2)]
            pair = [sb(ctx, f"pair{p}", [P, 2, TOPK, 2]) for p in range(2)]
            cntE = sb(ctx, "cntE", [E, 1])
            gtj = sb(ctx, "gtj", [E, 5])
            eT = sb(ctx, "eT", [E, 3])
            gend = sb(ctx, "gend", [E, 1])
            m1, m2 = sb(ctx, "m1", [E, NCOL]), sb(ctx, "m2", [E, NCOL])
            tg = sb(ctx, "tg", [P, 4, 3])
            mT = sb(ctx, "mT", [P, 4, NCH])
            t8 = sb(ctx, "t8", [P, 4])
            t8b = sb(ctx, "t8b", [P, 4])
            tt = sb(ctx, "tt", [P, 4])
            cmp_ = sb(ctx, "cmp_", [P, 4, NCH])
            fq = sb(ctx, "fq", [P, 4])
            qf = [sb(ctx, f"qf{n}", [P, 4]) for n in range(4)]
            qi = [sb(ctx, f"qi{n}", [P, 4], i32) for n in range(4)]
            qs = [sb(ctx, f"qs{n}", [P, 4], i32) for n in range(3)]
            tabi = sb(ctx, "tabi", [P, 4, NF], i32)
            slot_s = sb(ctx, "slot_s", [P, 4, P, 2])

            H_ps = [ps(ctx, f"H_ps{i}") for i in range(2)]
            HT_ps = [ps(ctx, f"HT_ps{i}") for i in range(2)]
            xa_ps, lg_ps, pos_ps, misc_ps = (ps(ctx, n) for n in ("xa_ps", "lg_ps", "pos_ps", "misc_ps"))
            lg = lg_ps[:, 0:2 * E].rearrange("p (i e) -> p i e", i=2)
            pos = pos_ps[:, 0:2 * E].rearrange("p (i e) -> p i e", i=2)

            cst_loaded, shared_loaded, x_loaded = sem("cst_loaded"), sem("shared_loaded"), sem("x_loaded")
            slot_padded, zero_ready, y_zeroed = sem("slot_padded"), sem("zero_ready"), sem("y_zeroed")
            h_stored, ht_stored = sem("h_stored"), sem("ht_stored")
            w_hi, w_lo, cst_ready = sem("w_hi"), sem("w_lo"), sem("cst_ready")
            xh_ready, xl_ready = sem("xh_ready"), sem("xl_ready")
            xa_done, xam_ready, xah_ready, xal_ready = sem("xa_done"), sem("xam_ready"), sem("xah_ready"), sem("xal_ready")
            h_done, h_copied, ht_done, ht_copied = sem("h_done"), sem("h_copied"), sem("ht_done"), sem("ht_copied")
            lg_done, nm_ready, exp_done, m_ready, pos_done = (sem("lg_done"), sem("nm_ready"), sem("exp_done"),
                                                              sem("m_ready"), sem("pos_done"))
            scat_ready, scattered = sem("scat_ready"), [sem(f"scattered{p}") for p in range(2)]
            cnt_done, tiles_ready, first_done, hot_ready, tg_done = (sem("cnt_done"), sem("tiles_ready"), sem("first_done"),
                                                                    sem("hot_ready"), sem("tg_done"))
            eT_ready, tab_ready, tab_stored, tab_loaded = sem("eT_ready"), sem("tab_ready"), sem("tab_stored"), sem("tab_loaded")
            slot_loaded, slotT_done, idxT_ready = sem("slot_loaded"), sem("slotT_done"), sem("idxT_ready")
            sh_hi, sh_lo = sem("sh_hi"), sem("sh_lo")

            shared_pieces = []
            for k in range(KD):
                shared_pieces.append((shgh[:, k, :], shgl[:, k, :], sh_raw[:, k % 2, :], shg[:, k * 2 * FS:(k + 1) * 2 * FS]))
            for n, (f, m) in enumerate(((0, 2), (2, 2), (4, 1))):
                shared_pieces.append((shdh[:, f:f + m, :].rearrange("p f d -> p (f d)"),
                                      shdl[:, f:f + m, :].rearrange("p f d -> p (f d)"),
                                      sh_raw[:, n % 2, 0:m * D], shd0[:, f:f + m, :].rearrange("p f d -> p (f d)")))
            shared_pieces.append((shdh[0:64, 5, :], shdl[0:64, 5, :], sh_raw[0:64, 1, 0:D], shd1))

            def over_batches(eng, slot):
                slot(0, 0, True, False)
                with eng.Fori(0, BATCH // 2 - 1) as i:
                    slot(2 * i + 1, 1, False, False)
                    slot(2 * i + 2, 0, False, False)
                slot(BATCH - 1, 1, False, True)

            H_rows = H_d[0:TOK, :].rearrange("(b i p) d -> b p i d", i=2, p=P)

            with nc.Block() as block:
                @block.sync
                def _(sp):
                    for dst, src in ((c, cst), (wt_raw, WT), (at_raw, AT), (bt_raw, BT), (gw, gwT), (scl, scal),
                                     (idb, idx), (ident, cst[:, C_ID:C_ID + P])):
                        sp.dma_start(dst[:], src).then_inc(cst_loaded, 16)
                    sp.dma_start(xraw[0][:], xT[0]).then_inc(x_loaded, 16)
                    sp.wait_ge(x_loaded, 16)
                    sp.dma_start(xraw[1][:], xT[1]).then_inc(x_loaded, 16)
                    for n in range(NCOL // P):
                        sp.dma_start(slot_d[n * P * P:(n + 1) * P * P, :].rearrange("(q p) a -> q (p a)", p=P),
                                     pad).then_inc(slot_padded, 16)
                    sp.wait_ge(zero_ready, 1)
                    sp.dma_start(H_d[TOK:TOK + P, :], zero[:]).then_inc(y_zeroed, 16)
                    sp.dma_start(y_d.rearrange("(n p) d -> p n d", p=P),
                                 zero[:].unsqueeze(1).to_broadcast([P, TOK // P + 1, D])).then_inc(y_zeroed, 16)

                    def load_shared(n):
                        if n >= 1:
                            sp.wait_ge(shared_loaded, 16 * n)
                        if n >= 2:
                            sp.wait_ge(sh_lo, n - 1)
                        _, _, dst, src = shared_pieces[n]
                        sp.dma_start(dst, src).then_inc(shared_loaded, 16)

                    load_shared(0)
                    load_shared(1)

                    def store(b, par, half):
                        sp.wait_ge(h_copied, 2 * b + 2)
                        sp.dma_start(H_rows[b], H_s[:]).then_inc(h_stored, 16)
                        sp.wait_ge(ht_copied, 2 * b + 2)
                        sp.dma_start(HT_d[half, :, :, par * SEQ:(par + 1) * SEQ], HT_s[:]).then_inc(ht_stored, 16)

                    def load(b, par):
                        sp.wait_ge(xl_ready, b - 1)
                        sp.wait_ge(x_loaded, 16 * b)
                        sp.dma_start(xraw[par][:], xT[b]).then_inc(x_loaded, 16)

                    with sp.Fori(0, BATCH // 2 - 1) as i:
                        load(2 * i + 2, 0)
                        store(2 * i, 0, i)
                        load(2 * i + 3, 1)
                        store(2 * i + 1, 1, i)
                    store(BATCH - 2, 0, NG - 1)
                    store(BATCH - 1, 1, NG - 1)
                    sp.wait_ge(tab_ready, 1)
                    sp.dma_start(tab_d.rearrange("(b p) f -> p b f", p=P), tabi[:]).then_inc(tab_stored, 16)
                    sp.wait_ge(tab_stored, 16)
                    sp.dma_start(tab[:], tab_d.rearrange("(a n) f -> a (n f)", a=1)).then_inc(tab_loaded, 16)
                    for n in range(2, len(shared_pieces)):
                        load_shared(n)
                    for par in range(2):
                        sp.wait_ge(scattered[par], 16 * 2 * TOPK * (BATCH // 2))
                    sp.dma_start(slot_s[:].rearrange("q c p a -> q c (p a)"), slot_d.rearrange("(c q p) a -> q c (p a)", q=P, p=P)).then_inc(slot_loaded, 16)
                    sp.wait_ge(tab_loaded, 16)
                    sp.wait_ge(y_zeroed, 32)
                    sp.wait_ge(h_stored, 16 * BATCH)
                    sp.wait_ge(ht_stored, 16 * BATCH)

                @block.gpsimd
                def _(pool):
                    pool.wait_ge(slot_padded, 16 * (NCOL // P))

                    def scatter(b, par):
                        pool.wait_ge(scat_ready, b + 1)
                        hold(pool, "pool")
                        for i in range(2):
                            for k in range(TOPK):
                                n = i * TOPK + k
                                pool.indirect_dma_start(
                                    out=slot_d, out_offset=bass.IndirectOffsetOnAxis(ap=scI[par][:, n:n + 1], axis=0),
                                    in_=pair[par][:, i, k, :], in_offset=None,
                                    bounds_check=E * CAP - 1, oob_is_err=False).then_inc(scattered[par], 16)

                    with pool.Fori(0, BATCH // 2) as i:
                        scatter(2 * i, 0)
                        scatter(2 * i + 1, 1)

                @block.scalar
                def _(act):
                    act.wait_ge(cst_loaded, 16 * 8)
                    for dst, src in ((wth, wt_raw), (ath, at_raw), (bth, bt_raw)):
                        act.copy(dst[:], src[:]).then_inc(w_hi, 1)

                    def split_x(b, par, first):
                        act.wait_ge(x_loaded, 16 * (b + 1))
                        if not first:
                            act.wait_ge(h_done, 2 * (b - 1))
                        act.copy(xh[par][:], xraw[par][:]).then_inc(xh_ready, 1)

                    split_x(0, 0, True)

                    def slot(b, par, first, last):
                        act.wait_ge(xa_done, b + 1)
                        act.activation(xam[:], xa_ps[:, 0:SEQ], ACT.Copy, scale=amask[:, bass.ds(b, 1)]).then_inc(xam_ready, 1)
                        act.wait_ge(xam_ready, b + 1)
                        act.copy(xah[:], xam[:]).then_inc(xah_ready, 1)
                        if not last:
                            split_x(b + 1, 1 - par, first)
                        for i in range(2):
                            act.wait_ge(h_done, 2 * b + i + 1)
                            if not first and i == 0:
                                act.wait_ge(h_stored, 16 * b)
                            act.copy(H_s[:, i, :], H_ps[i][:]).then_inc(h_copied, 1)
                        for i in range(2):
                            act.wait_ge(ht_done, 2 * b + i + 1)
                            if not first and i == 0:
                                act.wait_ge(ht_stored, 16 * b)
                            act.copy(HT_s[:, :, i * P:(i + 1) * P],
                                     HT_ps[i][:].rearrange("p (k t) -> p k t", k=KD)).then_inc(ht_copied, 1)
                        act.wait_ge(nm_ready, b + 1)
                        for i in range(2):
                            act.activation(ex[:, i, :], lg[:, i, :], ACT.Exp, bias=nm[:, i:i + 1],
                                           accum_out=S[:, i:i + 1]).then_inc(exp_done, 1)

                    act.wait_ge(cst_ready, 1)
                    over_batches(act, slot)
                    for n, (hi, _, piece, _) in enumerate(shared_pieces):
                        act.wait_ge(shared_loaded, 16 * (n + 1))
                        act.copy(hi, piece).then_inc(sh_hi, 1)

                @block.vector
                def _(dve):
                    dve.memset(zero[:], 0.0).then_inc(zero_ready, 1)
                    dve.wait_ge(cst_loaded, 16 * 8)
                    pre = Steps(dve, "setup_step")
                    dve.tensor_copy(tri[:], c[:, C_TRI:C_TRI + P])
                    dve.tensor_copy(one[:], c[:, C_ONE:C_ONE + P])
                    dve.memset(acc[0][:, 0, :], 0.0)
                    pre.next(dve.tensor_copy(idf[:], idb[:]))
                    dve.tensor_scalar(amask[:], idf[:], c[:, C_AD:C_AD + 1], scl[:], ALU.is_equal, ALU.mult)
                    for par in range(2):
                        for i in range(2):
                            pre.next(dve.tensor_scalar(tokf[par][:, i:i + 1], c[:, C_P:C_P + 1],
                                                       float((2 * par + i) * P), None, ALU.add))
                    dve.sem_inc(cst_ready, 1)
                    for n, (dst, src, hi) in enumerate(((wtl, wt_raw, wth), (atl, at_raw, ath), (btl, bt_raw, bth))):
                        dve.wait_ge(w_hi, n + 1)
                        dve.tensor_tensor(dst[:], src[:], hi[:], ALU.subtract).then_inc(w_lo, 1)

                    def split_x(b, par):
                        dve.wait_ge(xh_ready, b + 1)
                        dve.tensor_tensor(xl[par][:], xraw[par][:], xh[par][:], ALU.subtract).then_inc(xl_ready, 1)

                    split_x(0, 0)
                    st = Steps(dve, "routing_step")
                    NPLACE, NROUTE = 7, 13

                    def place(b, par, base):
                        st.n = 0
                        dve.wait_ge(pos_done, b + 1)
                        st.next(dve.tensor_tensor(prod[:], hot[par][:], pos.unsqueeze(2).to_broadcast([P, 2, TOPK, E]), ALU.mult), base)
                        st.next(dve.tensor_reduce(pos6[:], prod[:], AX.X, ALU.add), base)
                        st.next(dve.scalar_tensor_tensor(dst6[:], pos6[:], float(CAP - 1), base6[par][:], ALU.min, ALU.add), base)
                        st.next(dve.tensor_scalar(over[:], pos6[:], float(CAP), DROP, ALU.is_ge, ALU.mult), base)
                        st.next(dve.tensor_tensor(sc6[:], over[:], dst6[:], ALU.add), base)

                    def publish(par, turn, base):
                        if turn is not None:
                            dve.wait_ge(scattered[par], 16 * 2 * TOPK * turn)
                            st.next(dve.tensor_scalar(tokf[par][:], tokf[par][:], float(4 * P), None, ALU.add), base)
                        else:
                            st.next(dve.tensor_scalar(tokf[par][:], tokf[par][:], 0.0, None, ALU.add), base)
                        dve.tensor_copy(pair[par][:, :, :, 0], tokf[par][:].unsqueeze(2).to_broadcast([P, 2, TOPK]))
                        dve.tensor_copy(pair[par][:, :, :, 1], w6[par][:])
                        st.next(dve.tensor_copy(scI[par][:], sc6[:].rearrange("p i k -> p (i k)")), base)
                        dve.sem_inc(scat_ready, 1)

                    def route(b, par, base):
                        dve.wait_ge(lg_done, b + 1)
                        dve.tensor_reduce(nm[:], lg, AX.X, ALU.max, negate=True).then_inc(nm_ready, 1)
                        dve.wait_ge(exp_done, 2 * b + 2)
                        st.next(dve.reciprocal(rS[:], S[:]), base)
                        st.next(dve.tensor_tensor(sc[:], ex[:], rS[:].unsqueeze(2).to_broadcast([P, 2, E]), ALU.mult), base)
                        for i in range(2):
                            hold(dve, "dve")
                            st.next(dve.max(top8[:, i, :], sc[:, i, :]), base)
                            hold(dve, "dve")
                            st.next(dve.max_index(ix8[:, i, :], top8[:, i, :], sc[:, i, :]), base)
                        st.next(dve.tensor_copy(ixf[:], ix8[:, :, 0:TOPK]), base)
                        st.next(dve.tensor_reduce(ssum[:], top8[:, :, 0:TOPK], AX.X, ALU.add), base)
                        st.next(dve.tensor_scalar(ssum[:], ssum[:], 1e-20, None, ALU.add), base)
                        st.next(dve.reciprocal(rsum[:], ssum[:]), base)
                        dve.tensor_tensor(w6[par][:], top8[:, :, 0:TOPK], rsum[:].unsqueeze(2).to_broadcast([P, 2, TOPK]), ALU.mult)
                        dve.tensor_scalar(base6[par][:], ixf[:], float(CAP), None, ALU.mult)
                        st.next(dve.tensor_tensor(
                            hot[par][:], c[:, C_IOTA:C_IOTA + E].unsqueeze(1).unsqueeze(1).to_broadcast([P, 2, TOPK, E]),
                            ixf[:].unsqueeze(3).to_broadcast([P, 2, TOPK, E]), ALU.is_equal), base)
                        with nc.allow_low_precision(reason="sums of whole numbers up to 32"):
                            st.next(dve.tensor_reduce(M[par][:], hot[par][:].rearrange("p i k e -> p i e k"), AX.X, ALU.add), base)
                            st.next(dve.tensor_tensor(acc[par][:, 1, :], acc[par][:, 0, :], M[par][:, 0, :], ALU.add), base)
                            dve.tensor_tensor(acc[1 - par][:, 0, :], acc[par][:, 1, :], M[par][:, 1, :],
                                              ALU.add).then_inc(m_ready, 1)

                    NST = NPLACE + NROUTE

                    def slot(b, par, first, last, turn=None):
                        base = 0 if first else NST * b - NPLACE
                        dve.wait_ge(xah_ready, b + 1)
                        dve.tensor_tensor(xal[:], xam[:], xah[:], ALU.subtract).then_inc(xal_ready, 1)
                        if not last:
                            split_x(b + 1, 1 - par)
                        st.n = 0
                        if not first:
                            place(b - 1, 1 - par, base)
                            publish(1 - par, turn, base)
                        route(b, par, base)
                        assert st.n == (NROUTE if first else NST)

                    slot(0, 0, True, False)
                    slot(1, 1, False, False)
                    slot(2, 0, False, False)
                    with dve.Fori(1, BATCH // 2 - 1) as i:
                        slot(2 * i + 1, 1, False, False, turn=i)
                        slot(2 * i + 2, 0, False, False, turn=i)
                    slot(BATCH - 1, 1, False, True, turn=BATCH // 2 - 1)
                    base = NST * BATCH - NPLACE
                    place(BATCH - 1, 1, base)
                    publish(1, BATCH // 2 - 1, base)

                    tb = Steps(dve, "table_step")
                    dve.wait_ge(cnt_done, 1)
                    tb.next(dve.tensor_copy(cntE[:], misc_ps[0:E, 0:1]))
                    for j in range(1, CT):
                        dve.tensor_scalar(gtj[:, j - 1:j], cntE[:], float(j * P), None, ALU.is_gt).then_inc(tb.sem, 1)
                        tb.n += 1
                    dve.wait_ge(tb.sem, tb.n)
                    tb.next(dve.tensor_reduce(eT[:, 0:1], gtj[:], AX.X, ALU.add))
                    tb.next(dve.tensor_scalar(eT[:, 0:1], eT[:, 0:1], 1.0, None, ALU.add))
                    dve.sem_inc(tiles_ready, 1)
                    dve.wait_ge(first_done, 1)
                    dve.tensor_copy(eT[:, 1:2], misc_ps[0:E, 1:2])
                    dve.tensor_copy(tot[:, 0:1], misc_ps[0:1, 2:3])
                    dve.tensor_scalar(tot[:, 1:2], misc_ps[0:1, 2:3], -3.0, None, ALU.add)
                    tb.next(dve.tensor_copy(eT[:, 2:3], c[0:E, C_E:C_E + 1]))
                    tb.next(dve.tensor_tensor(gend[:], eT[:, 0:1], eT[:, 1:2], ALU.add))
                    dve.tensor_scalar(m1[:], c[0:E, C_G:C_G + NCOL], gend[:], None, ALU.is_ge)
                    tb.next(dve.tensor_scalar(m2[:], c[0:E, C_G:C_G + NCOL], eT[:, 1:2], None, ALU.is_ge))
                    dve.tensor_tensor(m2[:], m2[:], m1[:], ALU.subtract).then_inc(hot_ready, 1)
                    dve.wait_ge(tg_done, 1)
                    tb.next(dve.tensor_copy(tg[:], misc_ps[:, 16:28].rearrange("p (b f) -> p b f", b=4)))
                    tb.next(dve.tensor_copy(bnd[:], misc_ps[0:1, 64:64 + E]))
                    T_, G_, E_ = tg[:, :, 0], tg[:, :, 1], tg[:, :, 2]
                    tb.next(dve.tensor_tensor(tt[:], c[:, C_TG:C_TG + 4], G_, ALU.subtract))
                    dve.tensor_scalar(t8[:], tt[:], 8.0, None, ALU.mult)
                    tb.next(dve.tensor_scalar(t8b[:], tt[:], 8.0, 8.0, ALU.mult, ALU.add))
                    tb.next(dve.tensor_tensor(mT[:], c[:, C_M:C_M + NCH].unsqueeze(1).to_broadcast([P, 4, NCH]),
                                              T_.unsqueeze(2).to_broadcast([P, 4, NCH]), ALU.mult))
                    for f, t in ((0, t8), (1, t8b)):
                        tb.next(dve.tensor_tensor(cmp_[:], t[:].unsqueeze(2).to_broadcast([P, 4, NCH]), mT[:], ALU.is_ge))
                        tb.next(dve.tensor_reduce(fq[:], cmp_[:], AX.X, ALU.add))
                        tb.next(dve.scalar_tensor_tensor(qf[f][:], E_, float(NCH), fq[:], ALU.mult, ALU.add))
                        tb.next(dve.tensor_scalar(qf[f][:], qf[f][:], float(NCH), None, ALU.add))
                    dve.tensor_scalar(qf[2][:], T_, 1.0, None, ALU.is_equal)
                    tb.next(dve.scalar_tensor_tensor(qf[3][:], E_, float(CT), tt[:], ALU.mult, ALU.add))
                    for f in range(3):
                        dve.tensor_copy(qi[f][:], qf[f][:]).then_inc(tb.sem, 1)
                    tb.n += 3
                    tb.next(dve.tensor_copy(tabi[:, :, T_COL], qf[3][:]))
                    dve.tensor_single_scalar(qs[0][:], qi[1][:], 10, ALU.logical_shift_left)
                    tb.next(dve.tensor_single_scalar(qs[1][:], qi[2][:], 20, ALU.logical_shift_left))
                    tb.next(dve.tensor_tensor(qs[2][:], qs[0][:], qs[1][:], ALU.bitwise_or))
                    dve.tensor_tensor(tabi[:, :, T_WORD], qs[2][:], qi[0][:], ALU.bitwise_or).then_inc(tab_ready, 1)

                    for n, (hi, lo, piece, _) in enumerate(shared_pieces):
                        dve.wait_ge(sh_hi, n + 1)
                        dve.tensor_tensor(lo, piece, hi, ALU.subtract).then_inc(sh_lo, 1)
                    dve.wait_ge(slotT_done, 1)
                    dve.tensor_copy(wT[:], lg_ps[:])
                    dve.tensor_copy(idxT[:], misc_ps[:]).then_inc(idxT_ready, 1)
                    dve.wait_ge(idxT_ready, 1)

                @block.tensor
                def _(pe):
                    pe.wait_ge(cst_ready, 1)
                    pe.wait_ge(w_lo, 3)

                    def place(b, par):
                        pe.wait_ge(m_ready, b + 1)
                        for i in range(2):
                            nc.tensor.matmul(pos[:, i, :], tri[:], M[par][:, i, :], start=True, stop=False)
                            last = nc.tensor.matmul(pos[:, i, :], one[:], acc[par][:, i, :], start=False, stop=True)
                        last.then_inc(pos_done, 1)

                    def slot(b, par, first, last_):
                        pe.wait_ge(xh_ready, b + 1)
                        pe.wait_ge(xl_ready, b + 1)
                        for k in range(KD):
                            last = split_mm(xa_ps[:, 0:SEQ], ath[:, k, :], atl[:, k, :], xh[par][:, k, :], xl[par][:, k, :],
                                            k == 0, k == KD - 1)
                        last.then_inc(xa_done, 1)
                        for i in range(2):
                            for k in range(KD):
                                split_mm(H_ps[i][:], xh[par][:, k, i * P:(i + 1) * P], xl[par][:, k, i * P:(i + 1) * P],
                                         wth[:, k, :], wtl[:, k, :], k == 0, False)
                        pe.wait_ge(xal_ready, b + 1)
                        for i in range(2):
                            split_mm(H_ps[i][:], xah[:, i * P:(i + 1) * P], xal[:, i * P:(i + 1) * P], bth[:], btl[:],
                                     False, True).then_inc(h_done, 1)
                        if not first:
                            place(b - 1, 1 - par)
                        for i in range(2):
                            pe.wait_ge(h_copied, 2 * b + i + 1)
                            for k in range(KD):
                                last = nc.tensor.transpose(HT_ps[i][:, k * P:(k + 1) * P], H_s[:, i, k * P:(k + 1) * P], ident[:])
                            last.then_inc(ht_done, 1)
                        for i in range(2):
                            pe.wait_ge(ht_copied, 2 * b + i + 1)
                            for k in range(KD):
                                last = nc.tensor.matmul(lg[:, i, :], HT_s[:, k, i * P:(i + 1) * P], gw[:, k, :],
                                                        start=(k == 0), stop=(k == KD - 1))
                        last.then_inc(lg_done, 1)

                    over_batches(pe, slot)
                    place(BATCH - 1, 1)
                    nc.tensor.matmul(misc_ps[0:E, 0:1], acc[0][:, 0, :], one[:, 0:1], start=True, stop=True).then_inc(cnt_done, 1)
                    pe.wait_ge(tiles_ready, 1)
                    nc.tensor.matmul(misc_ps[0:E, 1:2], c[0:E, C_TRI:C_TRI + E], eT[:, 0:1], start=True, stop=True)
                    nc.tensor.matmul(misc_ps[0:1, 2:3], c[0:E, C_ONE:C_ONE + 1], eT[:, 0:1], start=True, stop=True).then_inc(first_done, 1)
                    pe.wait_ge(hot_ready, 1)
                    for n in range(4):
                        last = nc.tensor.matmul(misc_ps[:, 16 + 3 * n:19 + 3 * n], m2[:, n * P:(n + 1) * P], eT[:],
                                                start=True, stop=True)
                    nc.tensor.matmul(misc_ps[0:1, 64:64 + E], gend[:], c[0:E, C_ID:C_ID + E], start=True, stop=True).then_inc(tg_done, 1)
                    pe.wait_ge(slot_loaded, 16)
                    pe.wait_ge(tab_ready, 1)
                    for n in range(4):
                        nc.tensor.transpose(misc_ps[:, n * P:(n + 1) * P], slot_s[:, n, :, 0], ident[:])
                        last = nc.tensor.transpose(lg_ps[:, n * P:(n + 1) * P], slot_s[:, n, :, 1], ident[:])
                    last.then_inc(slotT_done, 1)

        with ExitStack() as ctx:
            raw = sb(ctx, "w_raw", [P, 2, WROW])
            wh, wl = sb(ctx, "wh", [P, 2, WROW], f32r), sb(ctx, "wl", [P, 2, WROW], f32r)
            raw16, wh16, wl16 = (t[:].rearrange("p a (n c) -> p (a n) c", c=CH) for t in (raw, wh, wl))
            idxc = sb(ctx, "idxc", [P, 1], i32)
            xg = sb(ctx, "xg", [P, D])
            xgh, xgl = sb(ctx, "xgh", [P, D], f32r), sb(ctx, "xgl", [P, D], f32r)
            gs = sb(ctx, "gs", [P, F])
            hm = sb(ctx, "hm", [P, F])
            hh, hl = sb(ctx, "hh", [P, 3 * P], f32r), sb(ctx, "hl", [P, 3 * P], f32r)
            idxd = sb(ctx, "idxd", [P, 1], i32)
            eo = sb(ctx, "eo", [P, D])
            g_ps, u_ps, xt_ps, ht_ps, o_ps = (ps(ctx, n) for n in ("g_ps", "u_ps", "xt_ps", "ht_ps", "o_ps"))
            w_loaded, wh_ready, wl_ready = sem("w_loaded"), sem("wh_ready"), sem("wl_ready")
            idx_ready, xg_loaded, tx_done = sem("idx_ready"), sem("xg_loaded"), sem("tx_done")
            xgh_ready, xgl_ready, gu_done, silu_done = sem("xgh_ready"), sem("xgl_ready"), sem("gu_done"), sem("silu_done")
            hm_ready, th_done, hh_ready, hl_ready = sem("hm_ready"), sem("th_done"), sem("hh_ready"), sem("hl_ready")
            d_done, eo_ready, idxd_ready, added = sem("d_done"), sem("eo_ready"), sem("idxd_ready"), sem("added")

            def field(eng, g, f, lo, hi):
                return eng.value_load(tab[0:1, bass.ds(g * NF + f, 1)], min_val=lo, max_val=hi)

            def tiles(eng):
                return eng.value_load(tot[0:1, 0:1], min_val=E, max_val=E * CT)

            def last_tile(eng):
                return eng.value_load(tot[0:1, 1:2], min_val=E - 3, max_val=E * CT - 3) + 2

            with nc.Block() as block:
                @block.sync
                def _(sp):
                    def load_expert(e, par):
                        for n in range(NLD):
                            if not (isinstance(e, int) and e == 0 and n == 0):
                                sp.wait_ge(w_loaded, 16 * (NLD * e + n))
                            sp.dma_start(raw[:, par, n * LD:(n + 1) * LD], wE[e, :, n * LD:(n + 1) * LD]).then_inc(w_loaded, 16)

                    load_expert(0, 0)
                    load_expert(1, 1)
                    with sp.Fori(1, E // 2) as i:
                        for par in range(2):
                            sp.wait_ge(wl_ready, NCH * (2 * i + par - 1))
                            hold(sp, "sp")
                            load_expert(2 * i + par, par)
                    sp.wait_ge(w_loaded, 16 * NLD * E)
                    sp.sem_inc(w_loaded, 16 * NLD)

                @block.gpsimd
                def _(pool):
                    total = tiles(pool)

                    def gather(g, first):
                        col = field(pool, g, T_COL, 0, NCOL - 1)
                        if not first:
                            pool.wait_ge(xg_loaded, 16 * g)
                            pool.wait_ge(tx_done, g)
                        pool.tensor_copy(idxc[:], idxT[:, bass.ds(col, 1)]).then_inc(idx_ready, 1)
                        pool.wait_ge(idx_ready, g + 1)
                        hold(pool, "pool")
                        pool.indirect_dma_start(out=xg[:], out_offset=None, in_=H_d,
                                                in_offset=bass.IndirectOffsetOnAxis(ap=idxc[:], axis=0)).then_inc(xg_loaded, 16)

                    def add_rows(g, first):
                        col = field(pool, g, T_COL, 0, NCOL - 1)
                        if not first:
                            pool.wait_ge(added, 16 * g)
                        pool.tensor_copy(idxd[:], idxT[:, bass.ds(col, 1)]).then_inc(idxd_ready, 1)
                        pool.wait_ge(idxd_ready, g + 1)
                        pool.wait_ge(eo_ready, g + 1)
                        hold(pool, "pool")
                        pool.indirect_dma_start(out=y_d, out_offset=bass.IndirectOffsetOnAxis(ap=idxd[:], axis=0),
                                                in_=eo[:], in_offset=None, compute_op=ALU.add).then_inc(added, 16)

                    gather(0, True)
                    gather(1, False)
                    gather(2, False)
                    gather(3, False)
                    add_rows(0, True)
                    with pool.Fori(4, total + 1) as g:
                        gather(g, False)
                        add_rows(g - 3, False)
                    last = last_tile(pool)
                    for back in (1, 0):
                        add_rows(last - back, False)
                    pool.wait_ge(added, 16 * total)
                    hold(pool, "pool")

                @block.scalar
                def _(act):
                    total = tiles(act)
                    for q in range(NCH):
                        act.wait_ge(w_loaded, 16 * (q * NLD // NCH + 1))
                        act.copy(wh16[:, q, :], raw16[:, q, :]).then_inc(wh_ready, 1)

                    def rows_hi(g):
                        act.wait_ge(tx_done, g + 1)
                        act.copy(xgh[:], xt_ps[:]).then_inc(xgh_ready, 1)

                    rows_hi(0)

                    def split_weights(g, word, fresh):
                        qb = act.snap(word & 1023)
                        act.wait_ge(w_loaded, ((qb >> 3) + 1) * (16 * NLD))
                        if not fresh:
                            act.wait_ge(d_done, (word >> 20) + g)
                        with act.Fori(qb, (word >> 10) & 1023) as q:
                            act.copy(wh16[:, q % 16, :], raw16[:, q % 16, :]).then_inc(wh_ready, 1)

                    def slot(g, last=False):
                        act.wait_ge(gu_done, g + 1)
                        act.activation(gs[:], g_ps[:, 0:F], ACT.Silu).then_inc(silu_done, 1)
                        if not last:
                            rows_hi(g + 1)
                            word = field(act, g + 1, T_WORD, 0, (1 << 21) - 1)
                        act.wait_ge(th_done, g + 1)
                        act.copy(hh[:, 0:2 * P], ht_ps[:, 0:2 * P])
                        act.copy(hh[0:96, 2 * P:3 * P], ht_ps[0:96, 2 * P:3 * P]).then_inc(hh_ready, 1)
                        if not last:
                            split_weights(g + 1, word, False)

                    split_weights(0, field(act, 0, T_WORD, 0, (1 << 21) - 1), True)
                    slot(0)
                    with act.Fori(1, total - 1) as g:
                        slot(g)
                    slot(last_tile(act), True)

                @block.vector
                def _(dve):
                    total = tiles(dve)
                    dve.sem_inc(d_done, 1)
                    for q in range(NCH):
                        dve.wait_ge(wh_ready, q + 1)
                        dve.tensor_tensor(wl16[:, q, :], raw16[:, q, :], wh16[:, q, :], ALU.subtract).then_inc(wl_ready, 1)

                    def rows_lo(g):
                        dve.wait_ge(xgh_ready, g + 1)
                        dve.tensor_tensor(xgl[:], xt_ps[:], xgh[:], ALU.subtract).then_inc(xgl_ready, 1)

                    rows_lo(0)

                    def weigh(g, col, first):
                        dve.wait_ge(d_done, g + 2)
                        if not first:
                            dve.wait_ge(added, 16 * g)
                        dve.tensor_scalar(eo[:], o_ps[:], wT[:, bass.ds(col, 1)], None, ALU.mult).then_inc(eo_ready, 1)

                    def split_weights(word):
                        with dve.Fori(word & 1023, (word >> 10) & 1023) as q:
                            dve.wait_ge(wh_ready, q + 1)
                            dve.tensor_tensor(wl16[:, q % 16, :], raw16[:, q % 16, :], wh16[:, q % 16, :],
                                              ALU.subtract).then_inc(wl_ready, 1)

                    def slot(g, first, second=False, last=False):
                        dve.wait_ge(silu_done, g + 1)
                        dve.tensor_tensor(hm[:], gs[:], u_ps[:, 0:F], ALU.mult).then_inc(hm_ready, 1)
                        if not last:
                            rows_lo(g + 1)
                            word = field(dve, g + 1, T_WORD, 0, (1 << 21) - 1)
                        if not first:
                            weigh(g - 1, field(dve, g - 1, T_COL, 0, NCOL - 1), second)
                        dve.wait_ge(hh_ready, g + 1)
                        dve.tensor_tensor(hl[:, 0:2 * P], ht_ps[:, 0:2 * P], hh[:, 0:2 * P], ALU.subtract)
                        dve.tensor_tensor(hl[0:96, 2 * P:3 * P], ht_ps[0:96, 2 * P:3 * P], hh[0:96, 2 * P:3 * P],
                                          ALU.subtract).then_inc(hl_ready, 1)
                        if not last:
                            split_weights(word)

                    split_weights(field(dve, 0, T_WORD, 0, (1 << 21) - 1))
                    slot(0, True)
                    slot(1, False, True)
                    with dve.Fori(2, total - 1) as g:
                        slot(g, False)
                    last = last_tile(dve)
                    slot(last, False, last=True)
                    weigh(last, field(dve, last, T_COL, 0, NCOL - 1), False)

                @block.tensor
                def _(pe):
                    total = tiles(pe)

                    def transpose_rows(g):
                        pe.wait_ge(xg_loaded, 16 * (g + 1))
                        for k in range(KD):
                            last = nc.tensor.transpose(xt_ps[:, k * P:(k + 1) * P], xg[:, k * P:(k + 1) * P], ident[:])
                        last.then_inc(tx_done, 1)

                    def down(g, par):
                        pe.wait_ge(hh_ready, g + 1)
                        pe.wait_ge(hl_ready, g + 1)
                        for n, (f0, fw) in enumerate(FC):
                            o = DN0 + n * D
                            last = split_mm(o_ps[:], hh[0:fw, f0:f0 + P], hl[0:fw, f0:f0 + P],
                                            wh[0:fw, par, o:o + D], wl[0:fw, par, o:o + D], n == 0, n == len(FC) - 1)
                        last.then_inc(d_done, 1)

                    def gate_up(g, par):
                        pe.wait_ge(xgh_ready, g + 1)
                        pe.wait_ge(xgl_ready, g + 1)
                        for k in range(KD):
                            for o, dst in ((0, g_ps), (F, u_ps)):
                                a = GU0 + k * 2 * F + o
                                last = split_mm(dst[:, 0:F], xgh[:, k * P:(k + 1) * P], xgl[:, k * P:(k + 1) * P],
                                                wh[:, par, a:a + F], wl[:, par, a:a + F], k == 0, k == KD - 1)
                        last.then_inc(gu_done, 1)

                    def transpose_h(g):
                        pe.wait_ge(hm_ready, g + 1)
                        for n, (f0, fw) in enumerate(FC):
                            last = nc.tensor.transpose(ht_ps[0:fw, n * P:(n + 1) * P], hm[:, f0:f0 + fw], ident[:])
                        last.then_inc(th_done, 1)

                    def expert(e, par, g0, first=False):
                        pe.wait_ge(wl_ready, NCH * (e + 1))
                        gate_up(g0, par)
                        end = pe.value_load(bnd[0:1, bass.ds(e, 1)], min_val=1, max_val=E * CT)
                        transpose_rows(g0 + 1)
                        if not first:
                            down(g0 - 1, 1 - par)
                        transpose_h(g0)
                        with pe.If(end > g0 + 1):
                            with pe.Fori(g0 + 1, end) as g:
                                gate_up(g, par)
                                transpose_rows(g + 1)
                                down(g - 1, par)
                                transpose_h(g)
                        return end

                    transpose_rows(0)
                    expert(1, 1, expert(0, 0, 0, True))
                    with pe.Fori(1, E // 2) as i:
                        g0 = pe.value_load(bnd[0:1, bass.ds(2 * i - 1, 1)], min_val=1, max_val=E * CT)
                        expert(2 * i + 1, 1, expert(2 * i, 0, g0))
                    down(last_tile(pe), 1)

        with ExitStack() as ctx:
            ht_raw = sb(ctx, "ht_raw", [P, KD, GRP])
            hth, htl = sb(ctx, "hth", [P, KD, GRP], f32r), sb(ctx, "htl", [P, KD, GRP], f32r)
            sg = [sb(ctx, f"sg{p}", [P, GRP]) for p in range(2)]
            sm = [sb(ctx, f"sm{p}", [P, GRP]) for p in range(2)]
            smh, sml = sb(ctx, "smh", [P, 6, GRP], f32r), sb(ctx, "sml", [P, 6, GRP], f32r)
            xres = [sb(ctx, f"xres{p}", [P, 2, D]) for p in range(2)]
            y = [sb(ctx, f"y{p}", [P, D]) for p in range(2)]
            sg_ps = [ps(ctx, f"sg_ps{p}") for p in range(2)]
            su_ps = [ps(ctx, f"su_ps{p}") for p in range(2)]
            so_ps = [ps(ctx, f"so_ps{p}") for p in range(2)]
            htr_loaded, hth_ready, htl_ready = sem("htr_loaded"), sem("hth_ready"), sem("htl_ready")
            sgu_done, ssilu_done, sm_ready, smh_ready, sml_ready = (sem("sgu_done"), sem("ssilu_done"), sem("sm_ready"),
                                                                    sem("smh_ready"), sem("sml_ready"))
            so_done, so_free = sem("so_done"), sem("so_free")
            y_done, x_res, y_stored = sem("y_done"), sem("x_res"), sem("y_stored")
            NT = TOK // P
            x_rows = xn.rearrange("(n p) d -> n p d", p=P)
            y_rows = y_d[0:TOK, :].rearrange("(n p) d -> n p d", p=P)
            out_rows = out.rearrange("b (i p) d -> (b i) p d", p=P)

            with nc.Block() as block:
                @block.sync
                def _(sp):
                    sp.dma_start(ht_raw[:], HT_d[0]).then_inc(htr_loaded, 16)

                    def residual(j, par):
                        sp.dma_start(xres[par][:, 0, :], x_rows[j]).then_inc(x_res, 16)
                        sp.dma_start(xres[par][:, 1, :], y_rows[j]).then_inc(x_res, 16)

                    residual(0, 0)

                    def group(n, final):
                        for i in range(4):
                            j, par = 4 * n + i, i % 2
                            if not (final and i == 3):
                                sp.wait_ge(x_res, 32 * (j + 1))
                                if not (isinstance(n, int) and n == 0 and i == 0):
                                    sp.wait_ge(y_done, j)
                                    hold(sp, "sp")
                                residual(j + 1, 1 - par)
                            if i == 0 and not final:
                                sp.wait_ge(htl_ready, n + 1)
                                sp.dma_start(ht_raw[:], HT_d[n + 1]).then_inc(htr_loaded, 16)
                            sp.wait_ge(y_done, j + 1)
                            hold(sp, "sp")
                            if not (isinstance(n, int) and n == 0 and i == 0):
                                sp.wait_ge(y_stored, 16 * j)
                            sp.dma_start(out_rows[j], y[par][:]).then_inc(y_stored, 16)

                    group(0, False)
                    with sp.Fori(1, NG - 1) as n:
                        group(n, False)
                    group(NG - 1, True)
                    sp.wait_ge(y_stored, 16 * NT)

                @block.scalar
                def _(act):
                    def columns_hi(n, first):
                        act.wait_ge(htr_loaded, 16 * (n + 1))
                        if not first:
                            act.wait_ge(sgu_done, 6 * n)
                        act.copy(hth[:], ht_raw[:]).then_inc(hth_ready, 1)

                    columns_hi(0, True)

                    def group(n, first, last):
                        for f, (f0, fw) in enumerate(FSC):
                            act.wait_ge(sgu_done, 6 * n + f + 1)
                            if f >= 2 or not first:
                                act.wait_ge(sm_ready, 6 * n + f - 1)
                            act.activation(sg[f % 2][0:fw, :], sg_ps[f % 2][0:fw, :], ACT.Silu).then_inc(ssilu_done, 1)
                            if f == 0 and not first:
                                act.wait_ge(so_done, 4 * n)
                            act.wait_ge(sm_ready, 6 * n + f + 1)
                            act.copy(smh[0:fw, f, :], sm[f % 2][0:fw, :]).then_inc(smh_ready, 1)
                        if not last:
                            columns_hi(n + 1, False)

                    group(0, True, False)
                    with act.Fori(1, NG - 1) as n:
                        group(n, False, False)
                    group(NG - 1, False, True)

                @block.vector
                def _(dve):
                    dve.sem_inc(so_free, 2)
                    def columns_lo(n):
                        dve.wait_ge(hth_ready, n + 1)
                        dve.tensor_tensor(htl[:], ht_raw[:], hth[:], ALU.subtract).then_inc(htl_ready, 1)

                    columns_lo(0)

                    def combine(n, i, first):
                        j, par = 4 * n + i, i % 2
                        dve.wait_ge(so_done, j + 1)
                        dve.wait_ge(x_res, 32 * (j + 1))
                        if not (first and i < 2):
                            dve.wait_ge(y_stored, 16 * (j - 1))
                        dve.tensor_tensor(y[par][:], so_ps[par][:], xres[par][:, 0, :], ALU.add).then_inc(so_free, 1)
                        dve.wait_ge(so_free, j + 3)
                        dve.tensor_tensor(y[par][:], y[par][:], xres[par][:, 1, :], ALU.add).then_inc(y_done, 1)

                    def hidden(n):
                        for f, (f0, fw) in enumerate(FSC):
                            dve.wait_ge(ssilu_done, 6 * n + f + 1)
                            dve.tensor_tensor(sm[f % 2][0:fw, :], sg[f % 2][0:fw, :], su_ps[f % 2][0:fw, :],
                                              ALU.mult).then_inc(sm_ready, 1)
                            dve.wait_ge(smh_ready, 6 * n + f + 1)
                            dve.tensor_tensor(sml[0:fw, f, :], sm[f % 2][0:fw, :], smh[0:fw, f, :],
                                              ALU.subtract).then_inc(sml_ready, 1)

                    def group(n, first, last):
                        hidden(n)
                        if not last:
                            columns_lo(n + 1)
                        for i in range(4):
                            combine(n, i, first)

                    group(0, True, False)
                    with dve.Fori(1, NG - 1) as n:
                        group(n, False, False)
                    group(NG - 1, False, True)

                @block.tensor
                def _(pe):
                    def group(n, first):
                        pe.wait_ge(hth_ready, n + 1)
                        pe.wait_ge(htl_ready, n + 1)
                        for f, (f0, fw) in enumerate(FSC):
                            if f >= 2:
                                pe.wait_ge(sm_ready, 6 * n + f - 1)
                            for o, dst in ((0, sg_ps[f % 2]), (FS, su_ps[f % 2])):
                                for k in range(KD):
                                    a = o + f0
                                    last = split_mm(dst[0:fw, :], shgh[:, k, a:a + fw], shgl[:, k, a:a + fw],
                                                    hth[:, k, :], htl[:, k, :], k == 0, k == KD - 1)
                            last.then_inc(sgu_done, 1)
                        for i in range(4):
                            pe.wait_ge(so_free, 4 * n + i + 1)
                            for f, (f0, fw) in enumerate(FSC):
                                if i == 0:
                                    pe.wait_ge(sml_ready, 6 * n + f + 1)
                                last = split_mm(so_ps[i % 2][:], smh[0:fw, f, i * P:(i + 1) * P], sml[0:fw, f, i * P:(i + 1) * P],
                                                shdh[0:fw, f, :], shdl[0:fw, f, :], f == 0, f == 5)
                            last.then_inc(so_done, 1)

                    group(0, True)
                    with pe.Fori(1, NG) as n:
                        group(n, False)


def kernel(x, itok_B_0_6, L0_cond_W, L0_cond_A, L0_cond_Bm, L0_cond_scalings, L0_ffn_gate_w, L0_ffn_w_gate, L0_ffn_w_up,
           L0_ffn_w_down, L0_ffn_sh_gate, L0_ffn_sh_up, L0_ffn_sh_down):
    import numpy as np
    import concourse.bacc as bacc
    from concourse.bass_utils import run_bass_kernel_spmd as run

    def chunks(a):
        return a.T.reshape(KD, P, -1).transpose(1, 0, 2)

    cst = np.zeros((P, NCONST), np.float32)
    cst[:, C_ID:C_ID + P] = np.eye(P)
    cst[:, C_TRI:C_TRI + P] = np.triu(np.ones((P, P)), 1)
    cst[:, C_ONE:C_ONE + P] = 1
    cst[:, C_IOTA:C_IOTA + E] = np.arange(E)
    cst[:, C_G:C_G + NCOL] = np.arange(NCOL)
    cst[:, C_TG:C_TG + 4] = np.arange(4)[None] * P + np.arange(P)[:, None]
    cst[:, C_M:C_M + NCH] = np.arange(1, NCH + 1)
    cst[:, C_AD] = np.arange(P) // 16
    cst[:, C_P] = np.arange(P)
    cst[:, C_E] = np.arange(P)

    wgu = np.concatenate([L0_ffn_w_gate, L0_ffn_w_up], 1)
    wgu = wgu.transpose(0, 2, 1).reshape(E, KD, P, 2 * F).transpose(0, 2, 1, 3).reshape(E, P, KD * 2 * F)
    wdn = np.zeros((E, 3 * P, D), np.float32)
    wdn[:, :F] = L0_ffn_w_down.transpose(0, 2, 1)
    wdn = wdn.reshape(E, 3, P, D).transpose(0, 2, 1, 3).reshape(E, P, 3 * D)
    dn = L0_ffn_sh_down.T
    arrays = {
        "xT": x.transpose(0, 2, 1).reshape(BATCH, KD, P, SEQ).transpose(0, 2, 1, 3),
        "xn": x.reshape(TOK, D),
        "WT": chunks(L0_cond_W),
        "AT": chunks(L0_cond_A.reshape(P, D)),
        "BT": L0_cond_Bm.transpose(0, 2, 1).reshape(P, D),
        "scal": np.repeat(L0_cond_scalings, 16).reshape(P, 1),
        "idx": np.broadcast_to(itok_B_0_6.reshape(1, BATCH), (P, BATCH)),
        "gwT": chunks(L0_ffn_gate_w),
        "cst": cst,
        "pad": np.broadcast_to(np.stack([np.arange(TOK, TOK + P), np.zeros(P)], 1).astype(np.float32).reshape(1, 2 * P), (P, 2 * P)),
        "shg": chunks(np.concatenate([L0_ffn_sh_gate, L0_ffn_sh_up], 0)).reshape(P, -1),
        "shd0": dn[:5 * P].reshape(5, P, D).transpose(1, 0, 2),
        "shd1": dn[5 * P:],
        "wE": np.concatenate([wgu, wdn], 2),
    }
    arrays = {f"{k}_dram": np.ascontiguousarray(v) for k, v in arrays.items()}
    nc = bacc.Bacc("TRN2", target_bir_lowering=False, num_devices=1)
    args = [nc.dram_tensor(k, v.shape, mybir.dt.from_np(v.dtype), kind="ExternalInput").ap() for k, v in arrays.items()]
    out = nc.dram_tensor("out_dram", (BATCH, SEQ, D), mybir.dt.float32, kind="ExternalOutput").ap()
    moe_kernel(nc, *args, out)
    r = run(nc, [arrays], core_ids=[0])
    return r.results[0]["out_dram"]
```

```python
import concourse.bass as bass
from concourse import mybir
from contextlib import ExitStack

P = 128
TOK, D = 4096, 512
BATCH, SEQ = 16, 256
KD = D // P
E, TOPK = 64, 6
F = 352
FC = [(0, 128), (128, 128), (256, 96)]
FS = 704
FSC = [(c * P, min(P, FS - c * P)) for c in range(6)]
CAP = 2 * ((TOK * TOPK + E - 1) // E)
CT = CAP // P
NCOL = 512
WROW = KD * 2 * F + 3 * D
NCH = 8
CH = WROW // NCH
NLD = 4
LD = WROW // NLD
GU0, DN0 = 0, KD * 2 * F
GRP = 512
NG = TOK // GRP
DROP = 1048576.0

C_ID, C_TRI, C_ONE, C_IOTA, C_G, C_TG, C_M, C_AD, C_P = 0, 128, 256, 384, 448, 960, 964, 972, 973
C_E = 974
NCONST = 975

T_WORD, T_COL = range(2)
NF = 2


def moe_kernel(nc, xT, xn, WT, AT, BT, scal, idx, gwT, cst, pad, shg, shd0, shd1, wE, out):
    f32, f32r, bf16, i32, u32 = (mybir.dt.float32, mybir.dt.float32r, mybir.dt.bfloat16,
                                 mybir.dt.int32, mybir.dt.uint32)
    ALU, ACT, AX = mybir.AluOpType, mybir.ActivationFunctionType, mybir.AxisListType

    H_d = nc.dram_tensor("H_rows", (TOK + P, D), f32).ap()
    HT_d = nc.dram_tensor("H_cols", (NG, P, KD, GRP), f32).ap()
    slot_d = nc.dram_tensor("slot_token", (NCOL * P, 2), f32).ap()
    tab_d = nc.dram_tensor("tile_table", (NCOL, NF), i32).ap()

    top = ExitStack()
    with top:
        def sb(ctx, name, shape, dt=f32):
            return ctx.enter_context(nc.sbuf_tensor(name, shape, dt))

        def ps(ctx, name, shape=(P, 512), dt=f32):
            return ctx.enter_context(nc.psum_tensor(name, list(shape), dt))

        def sem(name):
            return top.enter_context(nc.semaphore(name))

        waits_passed = {n: sem(f"waits_passed_{n}") for n in ("sp", "act", "dve", "pool")}

        def hold(eng, name):
            eng.sem_inc(waits_passed[name], 1)

        class Steps:

            def __init__(self, eng, name):
                self.eng, self.sem, self.n = eng, sem(name), 0

            def next(self, ins, base=0):
                self.n += 1
                ins.then_inc(self.sem, 1)
                self.eng.wait_ge(self.sem, base + self.n)

        w_raw = sb(top, "w_raw", [P, 2 * WROW])
        ident = sb(top, "ident", [P, P])
        idxT = sb(top, "idxT", [P, NCOL], i32)
        wT = sb(top, "wT", [P, NCOL])
        tab = sb(top, "tab", [1, NCOL * NF], i32)
        bnd = sb(top, "bnd", [1, E], i32)
        tot = sb(top, "tot", [1, 2], i32)

        w_loaded = sem("w_loaded")

        def load_expert(sp, e, par):
            for n in range(NLD):
                if not (isinstance(e, int) and e == 0 and n == 0):
                    sp.wait_ge(w_loaded, 16 * (NLD * e + n))
                a = par * WROW + n * LD
                sp.dma_start(w_raw[:, a:a + LD], wE[e, :, n * LD:(n + 1) * LD]).then_inc(w_loaded, 16)

        def split_mm(out_, lh, ll, rh, rl, first, last):
            nc.tensor.matmul(out_, lh, rh, start=first, stop=False)
            nc.tensor.matmul(out_, lh, rl, start=False, stop=False)
            return nc.tensor.matmul(out_, ll, rh, start=False, stop=last)

        with ExitStack() as ctx:
            c = sb(ctx, "cst", [P, NCONST])
            wt_raw = sb(ctx, "wt_raw", [P, KD, D])
            sh_raw = w_raw[:, 0:4 * FS].rearrange("p (a n) -> p a n", a=2)
            o = 4 * FS
            at_raw = w_raw[:, o:o + D].rearrange("p (k n) -> p k n", k=KD)
            bt_raw = w_raw[:, o + D:o + 2 * D]
            m1, m2 = w_raw[0:E, o + 2 * D:o + 2 * D + NCOL], w_raw[0:E, o + 2 * D + NCOL:o + 2 * D + 2 * NCOL]
            slot_s = w_raw[:, WROW + NCOL:WROW + NCOL + 8 * P].rearrange("p (c q a) -> p c q a", c=4, a=2)
            prod = w_raw[:, 6144:6144 + 2 * TOPK * E].rearrange("p (i k e) -> p i k e", i=2, k=TOPK)
            shgh = sb(ctx, "shgh", [P, KD, 2 * FS], f32r)
            shgl = sb(ctx, "shgl", [P, KD, 2 * FS], f32r)
            shdh = sb(ctx, "shdh", [P, 6, D], f32r)
            shdl = sb(ctx, "shdl", [P, 6, D], f32r)
            gw = sb(ctx, "gw", [P, KD, E])
            scl = sb(ctx, "scl", [P, 1])
            idb = sb(ctx, "idb", [P, BATCH], i32)
            wth, wtl = sb(ctx, "wth", [P, KD, D], f32r), sb(ctx, "wtl", [P, KD, D], f32r)
            ath, atl = sb(ctx, "ath", [P, KD, P], f32r), sb(ctx, "atl", [P, KD, P], f32r)
            bth, btl = sb(ctx, "bth", [P, D], f32r), sb(ctx, "btl", [P, D], f32r)
            idf = sb(ctx, "idf", [P, BATCH])
            amask = sb(ctx, "amask", [P, BATCH])
            tri = sb(ctx, "tri", [P, P], bf16)
            one = sb(ctx, "one", [P, P], bf16)
            zero = sb(ctx, "zero", [P, D])
            xraw = [sb(ctx, f"xraw{p}", [P, KD, SEQ]) for p in range(2)]
            smh, sml = sb(ctx, "smh", [P, 6, GRP], f32r), sb(ctx, "sml", [P, 6, GRP], f32r)
            xh, xl = ([t[:, 2 * p:2 * p + 2, :].rearrange("p a (b n) -> p (a b) n", b=2) for p in range(2)]
                      for t in (smh, sml))
            xam = sb(ctx, "xam", [P, SEQ])
            xah, xal = sb(ctx, "xah", [P, SEQ], f32r), sb(ctx, "xal", [P, SEQ], f32r)
            H_s = sb(ctx, "H_s", [P, 2, D])
            HT_s = sb(ctx, "HT_s", [P, KD, SEQ])
            nm = sb(ctx, "nm", [P, 2])
            ex = sb(ctx, "ex", [P, 2, E])
            S = sb(ctx, "S", [P, 2])
            rS = sb(ctx, "rS", [P, 2])
            sc = sb(ctx, "sc", [P, 2, E])
            top8 = sb(ctx, "top8", [P, 2, 8])
            ix8 = sb(ctx, "ix8", [P, 2, 8], u32)
            ixf = sb(ctx, "ixf", [P, 2, TOPK])
            ssum = sb(ctx, "ssum", [P, 2])
            rsum = sb(ctx, "rsum", [P, 2])
            base6 = [sb(ctx, f"base6{p}", [P, 2, TOPK]) for p in range(2)]
            w6 = [sb(ctx, f"w6{p}", [P, 2, TOPK]) for p in range(2)]
            hot = [sb(ctx, f"hot{p}", [P, 2, TOPK, E]) for p in range(2)]
            M = [sb(ctx, f"M{p}", [P, 2, E], bf16) for p in range(2)]
            acc = [sb(ctx, f"acc{p}", [P, 2, E], bf16) for p in range(2)]
            pos6 = sb(ctx, "pos6", [P, 2, TOPK])
            dst6 = sb(ctx, "dst6", [P, 2, TOPK])
            over = sb(ctx, "over", [P, 2, TOPK])
            sc6 = sb(ctx, "sc6", [P, 2, TOPK])
            scI = sb(ctx, "scI", [P, BATCH * 2 * TOPK], i32)
            pair = sb(ctx, "pair", [P, BATCH * 2, TOPK, 2])
            scI_now = [sb(ctx, f"scI_now{p}", [P, 2 * TOPK], i32) for p in range(2)]
            pair_now = [sb(ctx, f"pair_now{p}", [P, 2, TOPK, 2]) for p in range(2)]
            tokf = [sb(ctx, f"tokf{p}", [P, 2]) for p in range(2)]
            cntE = sb(ctx, "cntE", [E, 1])
            gtj = sb(ctx, "gtj", [E, 5])
            eT = sb(ctx, "eT", [E, 3])
            gend = sb(ctx, "gend", [E, 1])
            tg = sb(ctx, "tg", [P, 4, 3])
            mT = sb(ctx, "mT", [P, 4, NCH])
            t8 = sb(ctx, "t8", [P, 4])
            t8b = sb(ctx, "t8b", [P, 4])
            tt = sb(ctx, "tt", [P, 4])
            cmp_ = sb(ctx, "cmp_", [P, 4, NCH])
            fq = sb(ctx, "fq", [P, 4])
            qf = [sb(ctx, f"qf{n}", [P, 4]) for n in range(4)]
            qi = [sb(ctx, f"qi{n}", [P, 4], i32) for n in range(4)]
            qs = [sb(ctx, f"qs{n}", [P, 4], i32) for n in range(3)]
            tabi = sb(ctx, "tabi", [P, 4, NF], i32)
            ht_raw, hth, htl = wt_raw, wth, wtl
            sg = [H_s[:, p, :] for p in range(2)]
            sm = [HT_s[:, 2 * p:2 * p + 2, :].rearrange("p a n -> p (a n)") for p in range(2)]
            xres = [xraw[p][:, 0:2, :].rearrange("p a n -> p (a n)") for p in range(2)]
            y = [xraw[p][:, 2:4, :].rearrange("p a n -> p (a n)") for p in range(2)]

            H_ps = [ps(ctx, f"H_ps{i}") for i in range(2)]
            HT_ps = [ps(ctx, f"HT_ps{i}") for i in range(2)]
            xa_ps, lg_ps, pos_ps, misc_ps = (ps(ctx, n) for n in ("xa_ps", "lg_ps", "pos_ps", "misc_ps"))
            sg_ps, su_ps, so_ps = H_ps, HT_ps, [xa_ps, pos_ps]
            lg = lg_ps[:, 0:2 * E].rearrange("p (i e) -> p i e", i=2)
            pos = pos_ps[:, 0:2 * E].rearrange("p (i e) -> p i e", i=2)

            cst_loaded, shared_loaded, x_loaded = sem("cst_loaded"), sem("shared_loaded"), sem("x_loaded")
            slot_padded, zero_ready, pad_stored = sem("slot_padded"), sem("zero_ready"), sem("pad_stored")
            h_stored, ht_stored = sem("h_stored"), sem("ht_stored")
            w_hi, w_lo, cst_ready = sem("w_hi"), sem("w_lo"), sem("cst_ready")
            xh_ready, xl_ready = sem("xh_ready"), sem("xl_ready")
            xa_done, xam_ready, xah_ready, xal_ready = sem("xa_done"), sem("xam_ready"), sem("xah_ready"), sem("xal_ready")
            h_done, h_copied, ht_done, ht_copied = sem("h_done"), sem("h_copied"), sem("ht_done"), sem("ht_copied")
            lg_done, nm_ready, exp_done, m_ready, pos_done = (sem("lg_done"), sem("nm_ready"), sem("exp_done"),
                                                              sem("m_ready"), sem("pos_done"))
            scat_ready, scattered = sem("scat_ready"), [sem(f"scattered{p}") for p in range(2)]
            cnt_done, tiles_ready, first_done, hot_ready, tg_done = (sem("cnt_done"), sem("tiles_ready"), sem("first_done"),
                                                                    sem("hot_ready"), sem("tg_done"))
            eT_ready, tab_ready, tab_stored, tab_loaded = sem("eT_ready"), sem("tab_ready"), sem("tab_stored"), sem("tab_loaded")
            slot_loaded, slotT_done, idxT_ready = sem("slot_loaded"), sem("slotT_done"), sem("idxT_ready")
            sh_hi, sh_lo, picked = sem("sh_hi"), sem("sh_lo"), sem("picked")
            htr_loaded, hth_ready, htl_ready = sem("htr_loaded"), sem("hth_ready"), sem("htl_ready")
            sgu_done, ssilu_done, sm_ready, smh_ready, sml_ready = (sem("sgu_done"), sem("ssilu_done"), sem("sm_ready"),
                                                                    sem("smh_ready"), sem("sml_ready"))
            so_done, y_done, x_res, y_stored = sem("so_done"), sem("y_done"), sem("x_res"), sem("y_stored")

            shared_pieces = []
            for k in range(KD):
                shared_pieces.append((shgh[:, k, :], shgl[:, k, :], sh_raw[:, k % 2, :], shg[:, k * 2 * FS:(k + 1) * 2 * FS]))
            for n, (f, m) in enumerate(((0, 2), (2, 2), (4, 1))):
                shared_pieces.append((shdh[:, f:f + m, :].rearrange("p f d -> p (f d)"),
                                      shdl[:, f:f + m, :].rearrange("p f d -> p (f d)"),
                                      sh_raw[:, n % 2, 0:m * D], shd0[:, f:f + m, :].rearrange("p f d -> p (f d)")))
            shared_pieces.append((shdh[0:64, 5, :], shdl[0:64, 5, :], sh_raw[0:64, 1, 0:D], shd1))

            def over_batches(eng, slot):
                slot(0, 0, True, False)
                with eng.Fori(0, BATCH // 2 - 1) as i:
                    slot(2 * i + 1, 1, False, False)
                    slot(2 * i + 2, 0, False, False)
                slot(BATCH - 1, 1, False, True)

            def over_groups(eng, group):
                group(0, True, False)
                with eng.Fori(1, NG - 1) as n:
                    group(n, False, False)
                group(NG - 1, False, True)

            x_rows = xn.rearrange("(n p) d -> n p d", p=P)
            out_rows = out.rearrange("b (i p) d -> (b i) p d", p=P)
            H_rows = H_d[0:TOK, :].rearrange("(b i p) d -> b p i d", i=2, p=P)

            with nc.Block() as block:
                @block.sync
                def _(sp):
                    for dst, src in ((c, cst), (wt_raw, WT), (at_raw, AT), (bt_raw, BT), (gw, gwT), (scl, scal),
                                     (idb, idx), (ident, cst[:, C_ID:C_ID + P])):
                        sp.dma_start(dst[:], src).then_inc(cst_loaded, 16)
                    sp.dma_start(xraw[0][:], xT[0]).then_inc(x_loaded, 16)
                    sp.wait_ge(x_loaded, 16)
                    sp.dma_start(xraw[1][:], xT[1]).then_inc(x_loaded, 16)
                    for n in range(NCOL // P):
                        sp.dma_start(slot_d[n * P * P:(n + 1) * P * P, :].rearrange("(q p) a -> q (p a)", p=P),
                                     pad).then_inc(slot_padded, 16)
                    sp.wait_ge(zero_ready, 1)
                    sp.dma_start(H_d[TOK:TOK + P, :], zero[:]).then_inc(pad_stored, 16)

                    def store(b, par, half):
                        sp.wait_ge(h_copied, 2 * b + 2)
                        sp.dma_start(H_rows[b], H_s[:]).then_inc(h_stored, 16)
                        sp.wait_ge(ht_copied, 2 * b + 2)
                        sp.dma_start(HT_d[half, :, :, par * SEQ:(par + 1) * SEQ], HT_s[:]).then_inc(ht_stored, 16)

                    def load(b, par):
                        sp.wait_ge(xl_ready, b - 1)
                        sp.wait_ge(x_loaded, 16 * b)
                        sp.dma_start(xraw[par][:], xT[b]).then_inc(x_loaded, 16)

                    with sp.Fori(0, BATCH // 2 - 1) as i:
                        load(2 * i + 2, 0)
                        store(2 * i, 0, i)
                        load(2 * i + 3, 1)
                        store(2 * i + 1, 1, i)
                    sp.wait_ge(ht_stored, 16 * (BATCH - 2))
                    sp.dma_start(ht_raw[:], HT_d[0]).then_inc(htr_loaded, 16)
                    store(BATCH - 2, 0, NG - 1)
                    store(BATCH - 1, 1, NG - 1)
                    sp.wait_ge(xl_ready, BATCH)
                    sp.wait_ge(h_stored, 16 * BATCH)
                    sp.wait_ge(ht_stored, 16 * BATCH)

                    def residual(j, par):
                        sp.dma_start(xres[par], x_rows[j]).then_inc(x_res, 16)

                    residual(0, 0)

                    def group(n, first, last):
                        for i in range(4):
                            j, par = 4 * n + i, i % 2
                            if not (last and i == 3):
                                sp.wait_ge(x_res, 16 * (j + 1))
                                if not (first and i == 0):
                                    sp.wait_ge(y_done, j)
                                    hold(sp, "sp")
                                residual(j + 1, 1 - par)
                            if i == 0 and not last:
                                sp.wait_ge(htl_ready, n + 1)
                                sp.dma_start(ht_raw[:], HT_d[n + 1]).then_inc(htr_loaded, 16)
                            sp.wait_ge(y_done, j + 1)
                            hold(sp, "sp")
                            if not (first and i == 0):
                                sp.wait_ge(y_stored, 16 * j)
                            sp.dma_start(out_rows[j], y[par]).then_inc(y_stored, 16)

                    group(0, True, False)
                    sp.wait_ge(tab_ready, 1)
                    sp.dma_start(tab_d.rearrange("(b p) f -> p b f", p=P), tabi[:]).then_inc(tab_stored, 16)
                    sp.wait_ge(tab_stored, 16)
                    sp.dma_start(tab[:], tab_d.rearrange("(a n) f -> a (n f)", a=1)).then_inc(tab_loaded, 16)
                    with sp.Fori(1, NG - 1) as n:
                        group(n, False, False)
                    for par in range(2):
                        sp.wait_ge(scattered[par], 16 * 2 * TOPK * (BATCH // 2))
                    sp.dma_start(slot_s.rearrange("q c p a -> q c (p a)"),
                                 slot_d.rearrange("(c q p) a -> q c (p a)", q=P, p=P)).then_inc(slot_loaded, 16)
                    load_expert(sp, 0, 0)
                    group(NG - 1, False, True)
                    sp.wait_ge(tab_loaded, 16)
                    sp.wait_ge(pad_stored, 16)
                    sp.wait_ge(y_stored, 16 * (TOK // P))

                @block.gpsimd
                def _(pool):
                    def load_shared(n):
                        _, _, dst, src = shared_pieces[n]
                        pool.dma_start(dst, src).then_inc(shared_loaded, 16)

                    pool.wait_ge(cst_ready, 1)
                    load_shared(0)
                    for n, (hi, lo, piece, _) in enumerate(shared_pieces):
                        pool.wait_ge(shared_loaded, 16 * (n + 1))
                        if n + 1 < len(shared_pieces):
                            if n >= 1:
                                pool.wait_ge(sh_lo, n)
                            load_shared(n + 1)
                        pool.tensor_copy(hi, piece).then_inc(sh_hi, 1)
                        pool.wait_ge(sh_hi, n + 1)
                        pool.tensor_tensor(lo, piece, hi, ALU.subtract).then_inc(sh_lo, 1)

                    pool.wait_ge(slot_padded, 16 * (NCOL // P))

                    def scatter(b, par, turn):
                        pool.wait_ge(scat_ready, b + 1)
                        if turn is not None:
                            pool.wait_ge(scattered[par], 16 * 2 * TOPK * turn)
                        pool.tensor_copy(scI_now[par][:], scI[:, bass.ds(b * 2 * TOPK, 2 * TOPK)]).then_inc(picked, 1)
                        pool.tensor_copy(pair_now[par][:], pair[:, bass.ds(b * 2, 2), :, :]).then_inc(picked, 1)
                        pool.wait_ge(picked, 2 * b + 2)
                        hold(pool, "pool")
                        for i in range(2):
                            for k in range(TOPK):
                                n = i * TOPK + k
                                pool.indirect_dma_start(
                                    out=slot_d, out_offset=bass.IndirectOffsetOnAxis(ap=scI_now[par][:, n:n + 1], axis=0),
                                    in_=pair_now[par][:, i, k, :], in_offset=None,
                                    bounds_check=E * CAP - 1, oob_is_err=False).then_inc(scattered[par], 16)

                    for par in range(2):
                        scatter(par, par, None)
                    with pool.Fori(1, BATCH // 2) as i:
                        for par in range(2):
                            scatter(2 * i + par, par, i)

                @block.scalar
                def _(act):
                    act.wait_ge(cst_loaded, 16 * 8)
                    for dst, src in ((wth, wt_raw), (ath, at_raw), (bth, bt_raw)):
                        act.copy(dst[:], src[:]).then_inc(w_hi, 1)

                    def split_x(b, par, first):
                        act.wait_ge(x_loaded, 16 * (b + 1))
                        if not first:
                            act.wait_ge(h_done, 2 * (b - 1))
                        act.copy(xh[par][:], xraw[par][:]).then_inc(xh_ready, 1)

                    split_x(0, 0, True)

                    def slot(b, par, first, last):
                        act.wait_ge(xa_done, b + 1)
                        act.activation(xam[:], xa_ps[:, 0:SEQ], ACT.Copy, scale=amask[:, bass.ds(b, 1)]).then_inc(xam_ready, 1)
                        act.wait_ge(xam_ready, b + 1)
                        act.copy(xah[:], xam[:]).then_inc(xah_ready, 1)
                        if not last:
                            split_x(b + 1, 1 - par, first)
                        for i in range(2):
                            act.wait_ge(h_done, 2 * b + i + 1)
                            if not first and i == 0:
                                act.wait_ge(h_stored, 16 * b)
                            act.copy(H_s[:, i, :], H_ps[i][:]).then_inc(h_copied, 1)
                        for i in range(2):
                            act.wait_ge(ht_done, 2 * b + i + 1)
                            if not first and i == 0:
                                act.wait_ge(ht_stored, 16 * b)
                            act.copy(HT_s[:, :, i * P:(i + 1) * P],
                                     HT_ps[i][:].rearrange("p (k t) -> p k t", k=KD)).then_inc(ht_copied, 1)
                        if last:
                            columns_hi(0, True)
                        act.wait_ge(nm_ready, b + 1)
                        for i in range(2):
                            act.activation(ex[:, i, :], lg[:, i, :], ACT.Exp, bias=nm[:, i:i + 1],
                                           accum_out=S[:, i:i + 1]).then_inc(exp_done, 1)

                    def columns_hi(n, first):
                        act.wait_ge(htr_loaded, 16 * (n + 1))
                        if not first:
                            act.wait_ge(sgu_done, 6 * n)
                        act.copy(hth[:], ht_raw[:]).then_inc(hth_ready, 1)

                    def group(n, first, last):
                        for f, (f0, fw) in enumerate(FSC):
                            act.wait_ge(sgu_done, 6 * n + f + 1)
                            if f >= 2 or not first:
                                act.wait_ge(sm_ready, 6 * n + f - 1)
                            act.activation(sg[f % 2][0:fw, :], sg_ps[f % 2][0:fw, :], ACT.Silu).then_inc(ssilu_done, 1)
                            if f == 0 and not first:
                                act.wait_ge(so_done, 4 * n)
                            act.wait_ge(sm_ready, 6 * n + f + 1)
                            act.copy(smh[0:fw, f, :], sm[f % 2][0:fw, :]).then_inc(smh_ready, 1)
                        if not last:
                            columns_hi(n + 1, False)

                    act.wait_ge(cst_ready, 1)
                    over_batches(act, slot)
                    act.wait_ge(h_stored, 16 * BATCH)
                    over_groups(act, group)

                @block.vector
                def _(dve):
                    dve.memset(zero[:], 0.0).then_inc(zero_ready, 1)
                    dve.wait_ge(cst_loaded, 16 * 8)
                    pre = Steps(dve, "setup_step")
                    dve.tensor_copy(tri[:], c[:, C_TRI:C_TRI + P])
                    dve.tensor_copy(one[:], c[:, C_ONE:C_ONE + P])
                    dve.memset(acc[0][:, 0, :], 0.0)
                    pre.next(dve.tensor_copy(idf[:], idb[:]))
                    dve.tensor_scalar(amask[:], idf[:], c[:, C_AD:C_AD + 1], scl[:], ALU.is_equal, ALU.mult)
                    for par in range(2):
                        for i in range(2):
                            pre.next(dve.tensor_scalar(tokf[par][:, i:i + 1], c[:, C_P:C_P + 1],
                                                       float((2 * par + i - 4) * P), None, ALU.add))
                    dve.sem_inc(cst_ready, 1)
                    for n, (dst, src, hi) in enumerate(((wtl, wt_raw, wth), (atl, at_raw, ath), (btl, bt_raw, bth))):
                        dve.wait_ge(w_hi, n + 1)
                        dve.tensor_tensor(dst[:], src[:], hi[:], ALU.subtract).then_inc(w_lo, 1)

                    def split_x(b, par):
                        dve.wait_ge(xh_ready, b + 1)
                        dve.tensor_tensor(xl[par][:], xraw[par][:], xh[par][:], ALU.subtract).then_inc(xl_ready, 1)

                    split_x(0, 0)
                    st = Steps(dve, "routing_step")
                    NPLACE, NROUTE = 7, 13

                    def place(b, par, base):
                        st.n = 0
                        dve.wait_ge(pos_done, b + 1)
                        st.next(dve.tensor_tensor(prod[:], hot[par][:], pos.unsqueeze(2).to_broadcast([P, 2, TOPK, E]), ALU.mult), base)
                        st.next(dve.tensor_reduce(pos6[:], prod[:], AX.X, ALU.add), base)
                        st.next(dve.scalar_tensor_tensor(dst6[:], pos6[:], float(CAP - 1), base6[par][:], ALU.min, ALU.add), base)
                        st.next(dve.tensor_scalar(over[:], pos6[:], float(CAP), DROP, ALU.is_ge, ALU.mult), base)
                        st.next(dve.tensor_tensor(sc6[:], over[:], dst6[:], ALU.add), base)

                    def publish(b, par, base):
                        st.next(dve.tensor_scalar(tokf[par][:], tokf[par][:], float(4 * P), None, ALU.add), base)
                        to = pair[:, bass.ds(b * 2, 2), :, :]
                        dve.tensor_copy(to[:, :, :, 0], tokf[par][:].unsqueeze(2).to_broadcast([P, 2, TOPK]))
                        dve.tensor_copy(to[:, :, :, 1], w6[par][:])
                        st.next(dve.tensor_copy(scI[:, bass.ds(b * 2 * TOPK, 2 * TOPK)], sc6[:].rearrange("p i k -> p (i k)")), base)
                        dve.sem_inc(scat_ready, 1)

                    def route(b, par, base):
                        dve.wait_ge(lg_done, b + 1)
                        dve.tensor_reduce(nm[:], lg, AX.X, ALU.max, negate=True).then_inc(nm_ready, 1)
                        dve.wait_ge(exp_done, 2 * b + 2)
                        st.next(dve.reciprocal(rS[:], S[:]), base)
                        st.next(dve.tensor_tensor(sc[:], ex[:], rS[:].unsqueeze(2).to_broadcast([P, 2, E]), ALU.mult), base)
                        for i in range(2):
                            hold(dve, "dve")
                            st.next(dve.max(top8[:, i, :], sc[:, i, :]), base)
                            hold(dve, "dve")
                            st.next(dve.max_index(ix8[:, i, :], top8[:, i, :], sc[:, i, :]), base)
                        st.next(dve.tensor_copy(ixf[:], ix8[:, :, 0:TOPK]), base)
                        st.next(dve.tensor_reduce(ssum[:], top8[:, :, 0:TOPK], AX.X, ALU.add), base)
                        st.next(dve.tensor_scalar(ssum[:], ssum[:], 1e-20, None, ALU.add), base)
                        st.next(dve.reciprocal(rsum[:], ssum[:]), base)
                        dve.tensor_tensor(w6[par][:], top8[:, :, 0:TOPK], rsum[:].unsqueeze(2).to_broadcast([P, 2, TOPK]), ALU.mult)
                        dve.tensor_scalar(base6[par][:], ixf[:], float(CAP), None, ALU.mult)
                        st.next(dve.tensor_tensor(
                            hot[par][:], c[:, C_IOTA:C_IOTA + E].unsqueeze(1).unsqueeze(1).to_broadcast([P, 2, TOPK, E]),
                            ixf[:].unsqueeze(3).to_broadcast([P, 2, TOPK, E]), ALU.is_equal), base)
                        with nc.allow_low_precision(reason="sums of whole numbers up to 32"):
                            st.next(dve.tensor_reduce(M[par][:], hot[par][:].rearrange("p i k e -> p i e k"), AX.X, ALU.add), base)
                            st.next(dve.tensor_tensor(acc[par][:, 1, :], acc[par][:, 0, :], M[par][:, 0, :], ALU.add), base)
                            dve.tensor_tensor(acc[1 - par][:, 0, :], acc[par][:, 1, :], M[par][:, 1, :],
                                              ALU.add).then_inc(m_ready, 1)

                    NST = NPLACE + NROUTE

                    def columns_lo(n):
                        dve.wait_ge(hth_ready, n + 1)
                        dve.tensor_tensor(htl[:], ht_raw[:], hth[:], ALU.subtract).then_inc(htl_ready, 1)

                    def slot(b, par, first, last):
                        base = 0 if first else NST * b - NPLACE
                        dve.wait_ge(xah_ready, b + 1)
                        dve.tensor_tensor(xal[:], xam[:], xah[:], ALU.subtract).then_inc(xal_ready, 1)
                        if not last:
                            split_x(b + 1, 1 - par)
                        st.n = 0
                        if not first:
                            place(b - 1, 1 - par, base)
                            publish(b - 1, 1 - par, base)
                        if last:
                            columns_lo(0)
                        route(b, par, base)
                        assert st.n == (NROUTE if first else NST)

                    over_batches(dve, slot)

                    def combine(n, i, first):
                        j, par = 4 * n + i, i % 2
                        dve.wait_ge(so_done, j + 1)
                        dve.wait_ge(x_res, 16 * (j + 1))
                        if not (first and i < 2):
                            dve.wait_ge(y_stored, 16 * (j - 1))
                        dve.tensor_tensor(y[par], so_ps[par][:], xres[par], ALU.add).then_inc(y_done, 1)

                    def hidden(n, f, fw):
                        dve.wait_ge(ssilu_done, 6 * n + f + 1)
                        dve.tensor_tensor(sm[f % 2][0:fw, :], sg[f % 2][0:fw, :], su_ps[f % 2][0:fw, :],
                                          ALU.mult).then_inc(sm_ready, 1)
                        dve.wait_ge(smh_ready, 6 * n + f + 1)
                        dve.tensor_tensor(sml[0:fw, f, :], sm[f % 2][0:fw, :], smh[0:fw, f, :],
                                          ALU.subtract).then_inc(sml_ready, 1)

                    def group(n, first, last):
                        for f, (f0, fw) in enumerate(FSC):
                            hidden(n, f, fw)
                            if first and f == 1:
                                base = NST * BATCH - NPLACE
                                place(BATCH - 1, 1, base)
                                publish(BATCH - 1, 1, base)
                                count_tiles()
                        if first:
                            own_tiles()
                        if last:
                            dve.wait_ge(slotT_done, 1)
                            dve.tensor_copy(wT[:], lg_ps[:])
                            dve.tensor_copy(idxT[:], misc_ps[:]).then_inc(idxT_ready, 1)
                        else:
                            columns_lo(n + 1)
                        for i in range(4):
                            combine(n, i, first)
                        if first:
                            tile_table()

                    tb = Steps(dve, "table_step")

                    def count_tiles():
                        dve.wait_ge(cnt_done, 1)
                        tb.next(dve.tensor_copy(cntE[:], misc_ps[0:E, 0:1]))
                        for j in range(1, CT):
                            dve.tensor_scalar(gtj[:, j - 1:j], cntE[:], float(j * P), None, ALU.is_gt).then_inc(tb.sem, 1)
                            tb.n += 1
                        dve.wait_ge(tb.sem, tb.n)
                        tb.next(dve.tensor_reduce(eT[:, 0:1], gtj[:], AX.X, ALU.add))
                        tb.next(dve.tensor_scalar(eT[:, 0:1], eT[:, 0:1], 1.0, None, ALU.add))
                        dve.sem_inc(tiles_ready, 1)

                    def own_tiles():
                        dve.wait_ge(first_done, 1)
                        dve.tensor_copy(eT[:, 1:2], misc_ps[0:E, 1:2])
                        dve.tensor_copy(tot[:, 0:1], misc_ps[0:1, 2:3])
                        dve.tensor_scalar(tot[:, 1:2], misc_ps[0:1, 2:3], -3.0, None, ALU.add)
                        tb.next(dve.tensor_copy(eT[:, 2:3], c[0:E, C_E:C_E + 1]))
                        tb.next(dve.tensor_tensor(gend[:], eT[:, 0:1], eT[:, 1:2], ALU.add))
                        dve.tensor_scalar(m1[:], c[0:E, C_G:C_G + NCOL], gend[:], None, ALU.is_ge)
                        tb.next(dve.tensor_scalar(m2[:], c[0:E, C_G:C_G + NCOL], eT[:, 1:2], None, ALU.is_ge))
                        dve.tensor_tensor(m2[:], m2[:], m1[:], ALU.subtract).then_inc(hot_ready, 1)

                    def tile_table():
                        dve.wait_ge(tg_done, 1)
                        tb.next(dve.tensor_copy(tg[:], misc_ps[:, 16:28].rearrange("p (b f) -> p b f", b=4)))
                        tb.next(dve.tensor_copy(bnd[:], misc_ps[0:1, 64:64 + E]))
                        T_, G_, E_ = tg[:, :, 0], tg[:, :, 1], tg[:, :, 2]
                        tb.next(dve.tensor_tensor(tt[:], c[:, C_TG:C_TG + 4], G_, ALU.subtract))
                        dve.tensor_scalar(t8[:], tt[:], 8.0, None, ALU.mult)
                        tb.next(dve.tensor_scalar(t8b[:], tt[:], 8.0, 8.0, ALU.mult, ALU.add))
                        tb.next(dve.tensor_tensor(mT[:], c[:, C_M:C_M + NCH].unsqueeze(1).to_broadcast([P, 4, NCH]),
                                                  T_.unsqueeze(2).to_broadcast([P, 4, NCH]), ALU.mult))
                        for f, t in ((0, t8), (1, t8b)):
                            tb.next(dve.tensor_tensor(cmp_[:], t[:].unsqueeze(2).to_broadcast([P, 4, NCH]), mT[:], ALU.is_ge))
                            tb.next(dve.tensor_reduce(fq[:], cmp_[:], AX.X, ALU.add))
                            tb.next(dve.scalar_tensor_tensor(qf[f][:], E_, float(NCH), fq[:], ALU.mult, ALU.add))
                            tb.next(dve.tensor_scalar(qf[f][:], qf[f][:], float(NCH), None, ALU.add))
                        dve.tensor_scalar(qf[2][:], T_, 1.0, None, ALU.is_equal)
                        tb.next(dve.scalar_tensor_tensor(qf[3][:], E_, float(CT), tt[:], ALU.mult, ALU.add))
                        for f in range(3):
                            dve.tensor_copy(qi[f][:], qf[f][:]).then_inc(tb.sem, 1)
                        tb.n += 3
                        tb.next(dve.tensor_copy(tabi[:, :, T_COL], qf[3][:]))
                        dve.tensor_single_scalar(qs[0][:], qi[1][:], 10, ALU.logical_shift_left)
                        tb.next(dve.tensor_single_scalar(qs[1][:], qi[2][:], 20, ALU.logical_shift_left))
                        tb.next(dve.tensor_tensor(qs[2][:], qs[0][:], qs[1][:], ALU.bitwise_or))
                        dve.tensor_tensor(tabi[:, :, T_WORD], qs[2][:], qi[0][:], ALU.bitwise_or).then_inc(tab_ready, 1)

                    dve.wait_ge(ht_stored, 16 * BATCH)
                    over_groups(dve, group)
                    dve.wait_ge(idxT_ready, 1)

                @block.tensor
                def _(pe):
                    pe.wait_ge(cst_ready, 1)
                    pe.wait_ge(w_lo, 3)

                    def place(b, par):
                        pe.wait_ge(m_ready, b + 1)
                        for i in range(2):
                            nc.tensor.matmul(pos[:, i, :], tri[:], M[par][:, i, :], start=True, stop=False)
                            last = nc.tensor.matmul(pos[:, i, :], one[:], acc[par][:, i, :], start=False, stop=True)
                        last.then_inc(pos_done, 1)

                    def slot(b, par, first, last_):
                        pe.wait_ge(xh_ready, b + 1)
                        pe.wait_ge(xl_ready, b + 1)
                        for k in range(KD):
                            last = split_mm(xa_ps[:, 0:SEQ], ath[:, k, :], atl[:, k, :], xh[par][:, k, :], xl[par][:, k, :],
                                            k == 0, k == KD - 1)
                        last.then_inc(xa_done, 1)
                        for i in range(2):
                            for k in range(KD):
                                split_mm(H_ps[i][:], xh[par][:, k, i * P:(i + 1) * P], xl[par][:, k, i * P:(i + 1) * P],
                                         wth[:, k, :], wtl[:, k, :], k == 0, False)
                        pe.wait_ge(xal_ready, b + 1)
                        for i in range(2):
                            split_mm(H_ps[i][:], xah[:, i * P:(i + 1) * P], xal[:, i * P:(i + 1) * P], bth[:], btl[:],
                                     False, True).then_inc(h_done, 1)
                        if not first:
                            place(b - 1, 1 - par)
                        for i in range(2):
                            pe.wait_ge(h_copied, 2 * b + i + 1)
                            for k in range(KD):
                                last = nc.tensor.transpose(HT_ps[i][:, k * P:(k + 1) * P], H_s[:, i, k * P:(k + 1) * P], ident[:])
                            last.then_inc(ht_done, 1)
                        for i in range(2):
                            pe.wait_ge(ht_copied, 2 * b + i + 1)
                            for k in range(KD):
                                last = nc.tensor.matmul(lg[:, i, :], HT_s[:, k, i * P:(i + 1) * P], gw[:, k, :],
                                                        start=(k == 0), stop=(k == KD - 1))
                        last.then_inc(lg_done, 1)

                    def group(n, first, last_):
                        pe.wait_ge(hth_ready, n + 1)
                        pe.wait_ge(htl_ready, n + 1)
                        for f, (f0, fw) in enumerate(FSC):
                            if first and f == 2:
                                place(BATCH - 1, 1)
                                nc.tensor.matmul(misc_ps[0:E, 0:1], acc[0][:, 0, :], one[:, 0:1],
                                                 start=True, stop=True).then_inc(cnt_done, 1)
                            if f >= 2 or not first:
                                pe.wait_ge(sm_ready, 6 * n + f - 1)
                            for o, dst in ((0, sg_ps[f % 2]), (FS, su_ps[f % 2])):
                                for k in range(KD):
                                    a = o + f0
                                    last = split_mm(dst[0:fw, :], shgh[:, k, a:a + fw], shgl[:, k, a:a + fw],
                                                    hth[:, k, :], htl[:, k, :], k == 0, k == KD - 1)
                            last.then_inc(sgu_done, 1)
                        if first:
                            pe.wait_ge(tiles_ready, 1)
                            nc.tensor.matmul(misc_ps[0:E, 1:2], c[0:E, C_TRI:C_TRI + E], eT[:, 0:1], start=True, stop=True)
                            nc.tensor.matmul(misc_ps[0:1, 2:3], c[0:E, C_ONE:C_ONE + 1], eT[:, 0:1],
                                             start=True, stop=True).then_inc(first_done, 1)
                            pe.wait_ge(scat_ready, BATCH)
                        if last_:
                            pe.wait_ge(slot_loaded, 16)
                            pe.wait_ge(tab_ready, 1)
                            for m in range(4):
                                nc.tensor.transpose(misc_ps[:, m * P:(m + 1) * P], slot_s[:, m, :, 0], ident[:])
                                last = nc.tensor.transpose(lg_ps[:, m * P:(m + 1) * P], slot_s[:, m, :, 1], ident[:])
                            last.then_inc(slotT_done, 1)
                        for i in range(4):
                            if not (first and i < 2):
                                pe.wait_ge(y_done, 4 * n + i - 1)
                            for f, (f0, fw) in enumerate(FSC):
                                if i == 0:
                                    pe.wait_ge(sml_ready, 6 * n + f + 1)
                                last = split_mm(so_ps[i % 2][:], smh[0:fw, f, i * P:(i + 1) * P], sml[0:fw, f, i * P:(i + 1) * P],
                                                shdh[0:fw, f, :], shdl[0:fw, f, :], f == 0, f == 5)
                            last.then_inc(so_done, 1)
                        if first:
                            pe.wait_ge(hot_ready, 1)
                            for m in range(4):
                                nc.tensor.matmul(misc_ps[:, 16 + 3 * m:19 + 3 * m], m2[:, m * P:(m + 1) * P], eT[:],
                                                 start=True, stop=True)
                            nc.tensor.matmul(misc_ps[0:1, 64:64 + E], gend[:], c[0:E, C_ID:C_ID + E],
                                             start=True, stop=True).then_inc(tg_done, 1)

                    over_batches(pe, slot)
                    pe.wait_ge(sh_lo, len(shared_pieces))
                    over_groups(pe, group)

        with ExitStack() as ctx:
            wh, wl = sb(ctx, "wh", [P, 2, WROW], f32r), sb(ctx, "wl", [P, 2, WROW], f32r)
            raw16 = w_raw[:].rearrange("p (n c) -> p n c", c=CH)
            wh16, wl16 = (t[:].rearrange("p a (n c) -> p (a n) c", c=CH) for t in (wh, wl))
            idxc = sb(ctx, "idxc", [P, 1], i32)
            xg = sb(ctx, "xg", [P, D])
            xgh, xgl = sb(ctx, "xgh", [P, D], f32r), sb(ctx, "xgl", [P, D], f32r)
            gs = sb(ctx, "gs", [P, F])
            hm = sb(ctx, "hm", [P, F])
            hh, hl = sb(ctx, "hh", [P, 3 * P], f32r), sb(ctx, "hl", [P, 3 * P], f32r)
            idxd = sb(ctx, "idxd", [P, 1], i32)
            eo = sb(ctx, "eo", [P, D])
            g_ps, u_ps, xt_ps, ht_ps, o_ps = (ps(ctx, n) for n in ("g_ps", "u_ps", "xt_ps", "ht_ps", "o_ps"))
            wh_ready, wl_ready = sem("wh_ready"), sem("wl_ready")
            idx_ready, xg_loaded, tx_done = sem("idx_ready"), sem("xg_loaded"), sem("tx_done")
            xgh_ready, xgl_ready, gu_done, silu_done = sem("xgh_ready"), sem("xgl_ready"), sem("gu_done"), sem("silu_done")
            hm_ready, th_done, hh_ready, hl_ready = sem("hm_ready"), sem("th_done"), sem("hh_ready"), sem("hl_ready")
            d_done, eo_ready, idxd_ready, added = sem("d_done"), sem("eo_ready"), sem("idxd_ready"), sem("added")

            out_sums = out.rearrange("b s d -> (b s) d")

            def field(eng, g, f, lo, hi):
                return eng.value_load(tab[0:1, bass.ds(g * NF + f, 1)], min_val=lo, max_val=hi)

            def tiles(eng):
                return eng.value_load(tot[0:1, 0:1], min_val=E, max_val=E * CT)

            def last_tile(eng):
                return eng.value_load(tot[0:1, 1:2], min_val=E - 3, max_val=E * CT - 3) + 2

            with nc.Block() as block:
                @block.sync
                def _(sp):
                    load_expert(sp, 1, 1)
                    with sp.Fori(1, E // 2) as i:
                        for par in range(2):
                            sp.wait_ge(wl_ready, NCH * (2 * i + par - 1))
                            hold(sp, "sp")
                            load_expert(sp, 2 * i + par, par)
                    sp.wait_ge(w_loaded, 16 * NLD * E)
                    sp.sem_inc(w_loaded, 16 * NLD)

                @block.gpsimd
                def _(pool):
                    total = tiles(pool)

                    def gather(g, first):
                        col = field(pool, g, T_COL, 0, NCOL - 1)
                        if not first:
                            pool.wait_ge(xg_loaded, 16 * g)
                            pool.wait_ge(tx_done, g)
                        pool.tensor_copy(idxc[:], idxT[:, bass.ds(col, 1)]).then_inc(idx_ready, 1)
                        pool.wait_ge(idx_ready, g + 1)
                        hold(pool, "pool")
                        pool.indirect_dma_start(out=xg[:], out_offset=None, in_=H_d,
                                                in_offset=bass.IndirectOffsetOnAxis(ap=idxc[:], axis=0)).then_inc(xg_loaded, 16)

                    def add_rows(g, first):
                        col = field(pool, g, T_COL, 0, NCOL - 1)
                        if not first:
                            pool.wait_ge(added, 16 * g)
                        pool.tensor_copy(idxd[:], idxT[:, bass.ds(col, 1)]).then_inc(idxd_ready, 1)
                        pool.wait_ge(idxd_ready, g + 1)
                        pool.wait_ge(eo_ready, g + 1)
                        hold(pool, "pool")
                        pool.indirect_dma_start(out=out_sums, out_offset=bass.IndirectOffsetOnAxis(ap=idxd[:], axis=0),
                                                in_=eo[:], in_offset=None, compute_op=ALU.add,
                                                bounds_check=TOK - 1, oob_is_err=False).then_inc(added, 16)

                    gather(0, True)
                    gather(1, False)
                    gather(2, False)
                    gather(3, False)
                    add_rows(0, True)
                    with pool.Fori(4, total + 1) as g:
                        gather(g, False)
                        add_rows(g - 3, False)
                    last = last_tile(pool)
                    for back in (1, 0):
                        add_rows(last - back, False)
                    pool.wait_ge(added, 16 * total)
                    hold(pool, "pool")

                @block.scalar
                def _(act):
                    total = tiles(act)
                    for q in range(NCH):
                        act.wait_ge(w_loaded, 16 * (q * NLD // NCH + 1))
                        act.copy(wh16[:, q, :], raw16[:, q, :]).then_inc(wh_ready, 1)

                    def rows_hi(g):
                        act.wait_ge(tx_done, g + 1)
                        act.copy(xgh[:], xt_ps[:]).then_inc(xgh_ready, 1)

                    rows_hi(0)

                    def split_weights(g, word, fresh):
                        qb = act.snap(word & 1023)
                        act.wait_ge(w_loaded, ((qb >> 3) + 1) * (16 * NLD))
                        if not fresh:
                            act.wait_ge(d_done, (word >> 20) + g)
                        with act.Fori(qb, (word >> 10) & 1023) as q:
                            act.copy(wh16[:, q % 16, :], raw16[:, q % 16, :]).then_inc(wh_ready, 1)

                    def slot(g, last=False):
                        act.wait_ge(gu_done, g + 1)
                        act.activation(gs[:], g_ps[:, 0:F], ACT.Silu).then_inc(silu_done, 1)
                        if not last:
                            rows_hi(g + 1)
                            word = field(act, g + 1, T_WORD, 0, (1 << 21) - 1)
                        act.wait_ge(th_done, g + 1)
                        act.copy(hh[:, 0:2 * P], ht_ps[:, 0:2 * P])
                        act.copy(hh[0:96, 2 * P:3 * P], ht_ps[0:96, 2 * P:3 * P]).then_inc(hh_ready, 1)
                        if not last:
                            split_weights(g + 1, word, False)

                    split_weights(0, field(act, 0, T_WORD, 0, (1 << 21) - 1), True)
                    slot(0)
                    with act.Fori(1, total - 1) as g:
                        slot(g)
                    slot(last_tile(act), True)

                @block.vector
                def _(dve):
                    total = tiles(dve)
                    dve.sem_inc(d_done, 1)
                    for q in range(NCH):
                        dve.wait_ge(wh_ready, q + 1)
                        dve.tensor_tensor(wl16[:, q, :], raw16[:, q, :], wh16[:, q, :], ALU.subtract).then_inc(wl_ready, 1)

                    def rows_lo(g):
                        dve.wait_ge(xgh_ready, g + 1)
                        dve.tensor_tensor(xgl[:], xt_ps[:], xgh[:], ALU.subtract).then_inc(xgl_ready, 1)

                    rows_lo(0)

                    def weigh(g, col, first):
                        dve.wait_ge(d_done, g + 2)
                        if not first:
                            dve.wait_ge(added, 16 * g)
                        dve.tensor_scalar(eo[:], o_ps[:], wT[:, bass.ds(col, 1)], None, ALU.mult).then_inc(eo_ready, 1)

                    def split_weights(word):
                        with dve.Fori(word & 1023, (word >> 10) & 1023) as q:
                            dve.wait_ge(wh_ready, q + 1)
                            dve.tensor_tensor(wl16[:, q % 16, :], raw16[:, q % 16, :], wh16[:, q % 16, :],
                                              ALU.subtract).then_inc(wl_ready, 1)

                    def slot(g, first, second=False, last=False):
                        dve.wait_ge(silu_done, g + 1)
                        dve.tensor_tensor(hm[:], gs[:], u_ps[:, 0:F], ALU.mult).then_inc(hm_ready, 1)
                        if not last:
                            rows_lo(g + 1)
                            word = field(dve, g + 1, T_WORD, 0, (1 << 21) - 1)
                        if not first:
                            weigh(g - 1, field(dve, g - 1, T_COL, 0, NCOL - 1), second)
                        dve.wait_ge(hh_ready, g + 1)
                        dve.tensor_tensor(hl[:, 0:2 * P], ht_ps[:, 0:2 * P], hh[:, 0:2 * P], ALU.subtract)
                        dve.tensor_tensor(hl[0:96, 2 * P:3 * P], ht_ps[0:96, 2 * P:3 * P], hh[0:96, 2 * P:3 * P],
                                          ALU.subtract).then_inc(hl_ready, 1)
                        if not last:
                            split_weights(word)

                    split_weights(field(dve, 0, T_WORD, 0, (1 << 21) - 1))
                    slot(0, True)
                    slot(1, False, True)
                    with dve.Fori(2, total - 1) as g:
                        slot(g, False)
                    last = last_tile(dve)
                    slot(last, False, last=True)
                    weigh(last, field(dve, last, T_COL, 0, NCOL - 1), False)

                @block.tensor
                def _(pe):
                    total = tiles(pe)

                    def transpose_rows(g):
                        pe.wait_ge(xg_loaded, 16 * (g + 1))
                        for k in range(KD):
                            last = nc.tensor.transpose(xt_ps[:, k * P:(k + 1) * P], xg[:, k * P:(k + 1) * P], ident[:])
                        last.then_inc(tx_done, 1)

                    def down(g, par):
                        pe.wait_ge(hh_ready, g + 1)
                        pe.wait_ge(hl_ready, g + 1)
                        for n, (f0, fw) in enumerate(FC):
                            o = DN0 + n * D
                            last = split_mm(o_ps[:], hh[0:fw, f0:f0 + P], hl[0:fw, f0:f0 + P],
                                            wh[0:fw, par, o:o + D], wl[0:fw, par, o:o + D], n == 0, n == len(FC) - 1)
                        last.then_inc(d_done, 1)

                    def gate_up(g, par):
                        pe.wait_ge(xgh_ready, g + 1)
                        pe.wait_ge(xgl_ready, g + 1)
                        for k in range(KD):
                            for o, dst in ((0, g_ps), (F, u_ps)):
                                a = GU0 + k * 2 * F + o
                                last = split_mm(dst[:, 0:F], xgh[:, k * P:(k + 1) * P], xgl[:, k * P:(k + 1) * P],
                                                wh[:, par, a:a + F], wl[:, par, a:a + F], k == 0, k == KD - 1)
                        last.then_inc(gu_done, 1)

                    def transpose_h(g):
                        pe.wait_ge(hm_ready, g + 1)
                        for n, (f0, fw) in enumerate(FC):
                            last = nc.tensor.transpose(ht_ps[0:fw, n * P:(n + 1) * P], hm[:, f0:f0 + fw], ident[:])
                        last.then_inc(th_done, 1)

                    def expert(e, par, g0, first=False):
                        pe.wait_ge(wl_ready, NCH * (e + 1))
                        gate_up(g0, par)
                        end = pe.value_load(bnd[0:1, bass.ds(e, 1)], min_val=1, max_val=E * CT)
                        transpose_rows(g0 + 1)
                        if not first:
                            down(g0 - 1, 1 - par)
                        transpose_h(g0)
                        with pe.If(end > g0 + 1):
                            with pe.Fori(g0 + 1, end) as g:
                                gate_up(g, par)
                                transpose_rows(g + 1)
                                down(g - 1, par)
                                transpose_h(g)
                        return end

                    transpose_rows(0)
                    expert(1, 1, expert(0, 0, 0, True))
                    with pe.Fori(1, E // 2) as i:
                        g0 = pe.value_load(bnd[0:1, bass.ds(2 * i - 1, 1)], min_val=1, max_val=E * CT)
                        expert(2 * i + 1, 1, expert(2 * i, 0, g0))
                    down(last_tile(pe), 1)


def kernel(x, itok_B_0_6, L0_cond_W, L0_cond_A, L0_cond_Bm, L0_cond_scalings, L0_ffn_gate_w, L0_ffn_w_gate, L0_ffn_w_up,
           L0_ffn_w_down, L0_ffn_sh_gate, L0_ffn_sh_up, L0_ffn_sh_down):
    import numpy as np
    import concourse.bacc as bacc
    from concourse.bass_utils import run_bass_kernel_spmd as run

    def chunks(a):
        return a.T.reshape(KD, P, -1).transpose(1, 0, 2)

    cst = np.zeros((P, NCONST), np.float32)
    cst[:, C_ID:C_ID + P] = np.eye(P)
    cst[:, C_TRI:C_TRI + P] = np.triu(np.ones((P, P)), 1)
    cst[:, C_ONE:C_ONE + P] = 1
    cst[:, C_IOTA:C_IOTA + E] = np.arange(E)
    cst[:, C_G:C_G + NCOL] = np.arange(NCOL)
    cst[:, C_TG:C_TG + 4] = np.arange(4)[None] * P + np.arange(P)[:, None]
    cst[:, C_M:C_M + NCH] = np.arange(1, NCH + 1)
    cst[:, C_AD] = np.arange(P) // 16
    cst[:, C_P] = np.arange(P)
    cst[:, C_E] = np.arange(P)

    wgu = np.concatenate([L0_ffn_w_gate, L0_ffn_w_up], 1)
    wgu = wgu.transpose(0, 2, 1).reshape(E, KD, P, 2 * F).transpose(0, 2, 1, 3).reshape(E, P, KD * 2 * F)
    wdn = np.zeros((E, 3 * P, D), np.float32)
    wdn[:, :F] = L0_ffn_w_down.transpose(0, 2, 1)
    wdn = wdn.reshape(E, 3, P, D).transpose(0, 2, 1, 3).reshape(E, P, 3 * D)
    dn = L0_ffn_sh_down.T
    arrays = {
        "xT": x.transpose(0, 2, 1).reshape(BATCH, KD, P, SEQ).transpose(0, 2, 1, 3),
        "xn": x.reshape(TOK, D),
        "WT": chunks(L0_cond_W),
        "AT": chunks(L0_cond_A.reshape(P, D)),
        "BT": L0_cond_Bm.transpose(0, 2, 1).reshape(P, D),
        "scal": np.repeat(L0_cond_scalings, 16).reshape(P, 1),
        "idx": np.broadcast_to(itok_B_0_6.reshape(1, BATCH), (P, BATCH)),
        "gwT": chunks(L0_ffn_gate_w),
        "cst": cst,
        "pad": np.broadcast_to(np.stack([np.arange(TOK, TOK + P), np.zeros(P)], 1).astype(np.float32).reshape(1, 2 * P), (P, 2 * P)),
        "shg": chunks(np.concatenate([L0_ffn_sh_gate, L0_ffn_sh_up], 0)).reshape(P, -1),
        "shd0": dn[:5 * P].reshape(5, P, D).transpose(1, 0, 2),
        "shd1": dn[5 * P:],
        "wE": np.concatenate([wgu, wdn], 2),
    }
    arrays = {f"{k}_dram": np.ascontiguousarray(v) for k, v in arrays.items()}
    nc = bacc.Bacc("TRN2", target_bir_lowering=False, num_devices=1)
    args = [nc.dram_tensor(k, v.shape, mybir.dt.from_np(v.dtype), kind="ExternalInput").ap() for k, v in arrays.items()]
    out = nc.dram_tensor("out_dram", (BATCH, SEQ, D), mybir.dt.float32, kind="ExternalOutput").ap()
    moe_kernel(nc, *args, out)
    r = run(nc, [arrays], core_ids=[0])
    return r.results[0]["out_dram"]
```

```python
import concourse.bass as bass
from concourse import mybir
from contextlib import ExitStack

P = 128
TOK, D = 4096, 512
BATCH, SEQ = 16, 256
KD = D // P
E, TOPK = 64, 6
F = 352
FC = [(0, 128), (128, 128), (256, 96)]
FS = 704
FS5 = FS // P * P
FSC = [(c * P, min(P, FS - c * P)) for c in range(6)]
CAP = 2 * ((TOK * TOPK + E - 1) // E)
CT = CAP // P
NCOL = 512
WROW = KD * 2 * F + 3 * D
NCH = 8
CH = WROW // NCH
NLD = 4
LD = WROW // NLD
GU0, DN0 = 0, KD * 2 * F
GRP = 512
NG = TOK // GRP
DROP = 1048576.0

C_ID, C_TRI, C_ONE, C_IOTA, C_G, C_TG, C_M, C_AD, C_P = 0, 128, 256, 384, 448, 960, 964, 972, 973
C_E = 974
NCONST = 975

T_WORD, T_COL = range(2)
NF = 2


def moe_kernel(nc, xT, xn, WT, AT, BT, scal, idx, gwT, cst, pad, shg, shd, wE, out):
    f32, f32r, bf16, i32, u32 = (mybir.dt.float32, mybir.dt.float32r, mybir.dt.bfloat16,
                                 mybir.dt.int32, mybir.dt.uint32)
    ALU, ACT, AX = mybir.AluOpType, mybir.ActivationFunctionType, mybir.AxisListType

    H_d = nc.dram_tensor("H_rows", (TOK + P, D), f32).ap()
    HT_d = nc.dram_tensor("H_cols", (NG, P, KD, GRP), f32).ap()
    slot_d = nc.dram_tensor("slot_token", (NCOL * P, 2), f32).ap()
    tab_d = nc.dram_tensor("tile_table", (NCOL, NF), i32).ap()

    top = ExitStack()
    with top:
        def sb(ctx, name, shape, dt=f32):
            return ctx.enter_context(nc.sbuf_tensor(name, shape, dt))

        def ps(ctx, name, shape=(P, 512), dt=f32):
            return ctx.enter_context(nc.psum_tensor(name, list(shape), dt))

        def sem(name):
            return top.enter_context(nc.semaphore(name))

        waits_passed = {n: sem(f"waits_passed_{n}") for n in ("sp", "act", "dve", "pool")}

        def hold(eng, name):
            eng.sem_inc(waits_passed[name], 1)

        class Steps:

            def __init__(self, eng, name):
                self.eng, self.sem, self.n = eng, sem(name), 0

            def next(self, ins, base=0):
                self.n += 1
                ins.then_inc(self.sem, 1)
                self.eng.wait_ge(self.sem, base + self.n)

        w_raw = sb(top, "w_raw", [P, 2 * WROW])
        ident = sb(top, "ident", [P, P])
        idxT = sb(top, "idxT", [P, NCOL], i32)
        wT = sb(top, "wT", [P, NCOL])
        tab = sb(top, "tab", [1, NCOL * NF], i32)
        bnd = sb(top, "bnd", [1, E], i32)
        tot = sb(top, "tot", [1, 2], i32)

        wh, wl = sb(top, "wh", [P, 2 * WROW], f32r), sb(top, "wl", [P, 2 * WROW], f32r)
        raw16, wh16, wl16 = (t[:].rearrange("p (n c) -> p n c", c=CH) for t in (w_raw, wh, wl))
        xg = sb(top, "xg", [P, D])
        idxc = sb(top, "idxc", [P, 1], i32)
        w_loaded, wh_ready, wl_ready = sem("w_loaded"), sem("wh_ready"), sem("wl_ready")
        y_stored = sem("y_stored")
        idx_ready, xg_loaded = sem("idx_ready"), sem("xg_loaded")

        def load_expert(sp, e, par, parts=range(NLD)):
            for n in parts:
                if not (isinstance(e, int) and e == 0 and n == 0):
                    sp.wait_ge(w_loaded, 16 * (NLD * e + n))
                a = par * WROW + n * LD
                sp.dma_start(w_raw[:, a:a + LD], wE[e, :, n * LD:(n + 1) * LD]).then_inc(w_loaded, 16)

        def split_mm(out_, lh, ll, rh, rl, first, last):
            nc.tensor.matmul(out_, lh, rh, start=first, stop=False)
            nc.tensor.matmul(out_, lh, rl, start=False, stop=False)
            return nc.tensor.matmul(out_, ll, rh, start=False, stop=last)

        with ExitStack() as ctx:
            c = sb(ctx, "cst", [P, NCONST])
            wt_raw = sb(ctx, "wt_raw", [P, KD, D])
            sh_raw = w_raw[:, 0:4 * FS].rearrange("p (a n) -> p a n", a=2)
            o = 4 * FS
            at_raw = w_raw[:, o:o + D].rearrange("p (k n) -> p k n", k=KD)
            bt_raw = w_raw[:, o + D:o + 2 * D]
            m1, m2 = w_raw[0:E, o + 2 * D:o + 2 * D + NCOL], w_raw[0:E, o + 2 * D + NCOL:o + 2 * D + 2 * NCOL]
            o = WROW + NCOL
            slot_s = w_raw[:, o:o + 2 * NCOL].rearrange("p (c q a) -> p c q a", c=NCOL // P, a=2)
            o += 2 * NCOL
            prod = w_raw[:, o:o + 2 * TOPK * E].rearrange("p (i k e) -> p i k e", i=2, k=TOPK)
            o += 2 * TOPK * E
            zero = w_raw[:, o:o + D]
            up5 = w_raw[:, o + D:o + D + GRP]
            shgh, shgl = (t[:, 0:KD * 2 * FS].rearrange("p (k n) -> p k n", k=KD) for t in (wh, wl))
            shdh, shdl = (t[:, KD * 2 * FS:KD * 2 * FS + 6 * D].rearrange("p (f d) -> p f d", f=6) for t in (wh, wl))
            gw = sb(ctx, "gw", [P, KD, E])
            scl = sb(ctx, "scl", [P, 1])
            idb = sb(ctx, "idb", [P, BATCH], i32)
            wth, wtl = sb(ctx, "wth", [P, KD, D], f32r), sb(ctx, "wtl", [P, KD, D], f32r)
            ath, atl = sb(ctx, "ath", [P, KD, P], f32r), sb(ctx, "atl", [P, KD, P], f32r)
            bth, btl = sb(ctx, "bth", [P, D], f32r), sb(ctx, "btl", [P, D], f32r)
            idf = sb(ctx, "idf", [P, BATCH])
            amask = sb(ctx, "amask", [P, BATCH])
            tri = sb(ctx, "tri", [P, P], bf16)
            one = sb(ctx, "one", [P, P], bf16)
            xraw = [sb(ctx, f"xraw{p}", [P, KD, SEQ]) for p in range(2)]
            smh, sml = sb(ctx, "smh", [P, 6, GRP], f32r), sb(ctx, "sml", [P, 6, GRP], f32r)
            xh, xl = ([t[:, 2 * p:2 * p + 2, :].rearrange("p a (b n) -> p (a b) n", b=2) for p in range(2)]
                      for t in (smh, sml))
            xam = sb(ctx, "xam", [P, SEQ])
            xah, xal = sb(ctx, "xah", [P, SEQ], f32r), sb(ctx, "xal", [P, SEQ], f32r)
            H_s = sb(ctx, "H_s", [P, 2, D])
            HT_s = sb(ctx, "HT_s", [P, KD, SEQ])
            nm = sb(ctx, "nm", [P, 2])
            ex = sb(ctx, "ex", [P, 2, E])
            S = sb(ctx, "S", [P, 2])
            rS = sb(ctx, "rS", [P, 2])
            sc = sb(ctx, "sc", [P, 2, E])
            top8 = sb(ctx, "top8", [P, 2, 8])
            ix8 = sb(ctx, "ix8", [P, 2, 8], u32)
            ixf = sb(ctx, "ixf", [P, 2, TOPK])
            ssum = sb(ctx, "ssum", [P, 2])
            rsum = sb(ctx, "rsum", [P, 2])
            base6 = [sb(ctx, f"base6{p}", [P, 2, TOPK]) for p in range(2)]
            w6 = [sb(ctx, f"w6{p}", [P, 2, TOPK]) for p in range(2)]
            hot = [sb(ctx, f"hot{p}", [P, 2, TOPK, E]) for p in range(2)]
            M = [sb(ctx, f"M{p}", [P, 2, E], bf16) for p in range(2)]
            acc = [sb(ctx, f"acc{p}", [P, 2, E], bf16) for p in range(2)]
            pos6 = sb(ctx, "pos6", [P, 2, TOPK])
            dst6 = sb(ctx, "dst6", [P, 2, TOPK])
            over = sb(ctx, "over", [P, 2, TOPK])
            sc6 = sb(ctx, "sc6", [P, 2, TOPK])
            scI = sb(ctx, "scI", [P, BATCH * 2 * TOPK], i32)
            pair = sb(ctx, "pair", [P, BATCH * 2, TOPK, 2])
            scI_now = [sb(ctx, f"scI_now{p}", [P, 2 * TOPK], i32) for p in range(2)]
            pair_now = [sb(ctx, f"pair_now{p}", [P, 2, TOPK, 2]) for p in range(2)]
            tokf = [sb(ctx, f"tokf{p}", [P, 2]) for p in range(2)]
            cntE = sb(ctx, "cntE", [E, 1])
            gtj = sb(ctx, "gtj", [E, 5])
            eT = sb(ctx, "eT", [E, 3])
            gend = sb(ctx, "gend", [E, 1])
            tg = sb(ctx, "tg", [P, 4, 3])
            mT = sb(ctx, "mT", [P, 4, NCH])
            t8 = sb(ctx, "t8", [P, 4])
            t8b = sb(ctx, "t8b", [P, 4])
            tt = sb(ctx, "tt", [P, 4])
            cmp_ = sb(ctx, "cmp_", [P, 4, NCH])
            fq = sb(ctx, "fq", [P, 4])
            qf = [sb(ctx, f"qf{n}", [P, 4]) for n in range(4)]
            qi = [sb(ctx, f"qi{n}", [P, 4], i32) for n in range(4)]
            qs = [sb(ctx, f"qs{n}", [P, 4], i32) for n in range(3)]
            tabi = sb(ctx, "tabi", [P, 4, NF], i32)
            ht_raw, hth, htl = wt_raw, wth, wtl
            sg = [H_s[:, p, :] for p in range(2)]
            sm = [HT_s[:, 2 * p:2 * p + 2, :].rearrange("p a n -> p (a n)") for p in range(2)]
            xres = [xraw[p][:, 0:2, :].rearrange("p a n -> p (a n)") for p in range(2)]
            y = [xraw[p][:, 2:4, :].rearrange("p a n -> p (a n)") for p in range(2)]

            H_ps = [ps(ctx, f"H_ps{i}") for i in range(2)]
            HT_ps = [ps(ctx, f"HT_ps{i}") for i in range(2)]
            xa_ps, lg_ps, pos_ps, misc_ps = (ps(ctx, n) for n in ("xa_ps", "lg_ps", "pos_ps", "misc_ps"))
            sg_ps, su_ps, so_ps = H_ps, HT_ps, [xa_ps, pos_ps]
            lg = lg_ps[:, 0:2 * E].rearrange("p (i e) -> p i e", i=2)
            pos = pos_ps[:, 0:2 * E].rearrange("p (i e) -> p i e", i=2)

            at_loaded, wt_loaded = sem("at_loaded"), sem("wt_loaded")
            cst_loaded, shared_loaded, x_loaded = sem("cst_loaded"), sem("shared_loaded"), sem("x_loaded")
            slot_padded, zero_ready, pad_stored = sem("slot_padded"), sem("zero_ready"), sem("pad_stored")
            h_stored, ht_stored = sem("h_stored"), sem("ht_stored")
            w_hi, w_lo, cst_ready = sem("w_hi"), sem("w_lo"), sem("cst_ready")
            xh_ready, xl_ready = sem("xh_ready"), sem("xl_ready")
            xa_done, xam_ready, xah_ready, xal_ready = sem("xa_done"), sem("xam_ready"), sem("xah_ready"), sem("xal_ready")
            h_done, h_copied, ht_done, ht_copied = sem("h_done"), sem("h_copied"), sem("ht_done"), sem("ht_copied")
            lg_done, nm_ready, exp_done, m_ready, pos_done = (sem("lg_done"), sem("nm_ready"), sem("exp_done"),
                                                              sem("m_ready"), sem("pos_done"))
            scat_ready, scattered = sem("scat_ready"), [sem(f"scattered{p}") for p in range(2)]
            cnt_done, tiles_ready, first_done, hot_ready, tg_done = (sem("cnt_done"), sem("tiles_ready"), sem("first_done"),
                                                                    sem("hot_ready"), sem("tg_done"))
            tab_ready, tab_stored, tab_loaded = sem("tab_ready"), sem("tab_stored"), sem("tab_loaded")
            slot_loaded, slotT_done, idxT_ready = sem("slot_loaded"), sem("slotT_done"), sem("idxT_ready")
            sh_hi, sh_lo, picked = sem("sh_hi"), sem("sh_lo"), sem("picked")
            htr_loaded, hth_ready, htl_ready = sem("htr_loaded"), sem("hth_ready"), sem("htl_ready")
            sgu_done, ssilu_done, sm_ready, smh_ready, sml_ready = (sem("sgu_done"), sem("ssilu_done"), sem("sm_ready"),
                                                                    sem("smh_ready"), sem("sml_ready"))
            up_moved = sem("up_moved")
            so_done, y_done, x_res = sem("so_done"), sem("y_done"), sem("x_res")

            HALF = FSC[5][1]
            shared_pieces = []
            for k in range(KD):
                shared_pieces.append((shgh[:, k, :], shgl[:, k, :], sh_raw[:, k % 2, :], shg[:, k * 2 * FS:(k + 1) * 2 * FS]))
            for n, (f, m) in enumerate(((0, 2), (2, 2), (4, 2))):
                shared_pieces.append((shdh[:, f:f + m, :].rearrange("p f d -> p (f d)"),
                                      shdl[:, f:f + m, :].rearrange("p f d -> p (f d)"),
                                      sh_raw[:, n % 2, 0:m * D], shd[:, f:f + m, :].rearrange("p f d -> p (f d)")))

            def over_batches(eng, slot):
                slot(0, 0, True, 2)
                with eng.Fori(0, BATCH // 2 - 2) as i:
                    slot(2 * i + 1, 1, False, 2)
                    slot(2 * i + 2, 0, False, 2)
                slot(BATCH - 3, 1, False, 2)
                slot(BATCH - 2, 0, False, 1)
                slot(BATCH - 1, 1, False, 0)

            def over_groups(eng, group):
                group(0, True, False)
                with eng.Fori(1, NG - 1) as n:
                    group(n, False, False)
                group(NG - 1, False, True)

            x_rows = xn.rearrange("(n p) d -> n p d", p=P)
            out_rows = out.rearrange("(n p) d -> n p d", p=P)
            H_rows = H_d[0:TOK, :].rearrange("(b i p) d -> b p i d", i=2, p=P)

            with nc.Block() as block:
                @block.sync
                def _(sp):
                    sp.dma_start(at_raw, AT).then_inc(at_loaded, 16)
                    sp.dma_start(xraw[0][:], xT[0]).then_inc(x_loaded, 16)
                    sp.dma_start(wt_raw[:], WT).then_inc(wt_loaded, 16)
                    for dst, src in ((scl, scal), (idb, idx), (bt_raw, BT), (c, cst), (gw, gwT),
                                     (ident, cst[:, C_ID:C_ID + P])):
                        sp.dma_start(dst[:], src).then_inc(cst_loaded, 16)
                    sp.wait_ge(x_loaded, 16)
                    sp.dma_start(xraw[1][:], xT[1]).then_inc(x_loaded, 16)
                    for n in range(NCOL // P):
                        sp.dma_start(slot_d[n * P * P:(n + 1) * P * P, :].rearrange("(q p) a -> q (p a)", p=P),
                                     pad).then_inc(slot_padded, 16)
                    sp.wait_ge(zero_ready, 1)
                    for rows in (H_d, out):
                        sp.dma_start(rows[TOK:TOK + P, :], zero[:]).then_inc(pad_stored, 16)

                    def store(b, par, half):
                        sp.wait_ge(h_copied, 2 * b + 2)
                        sp.dma_start(H_rows[b], H_s[:]).then_inc(h_stored, 16)
                        sp.wait_ge(ht_copied, 2 * b + 2)
                        sp.dma_start(HT_d[half, :, :, par * SEQ:(par + 1) * SEQ], HT_s[:]).then_inc(ht_stored, 16)

                    def load(b, par):
                        sp.wait_ge(xl_ready, b - 1)
                        sp.wait_ge(x_loaded, 16 * b)
                        sp.dma_start(xraw[par][:], xT[b]).then_inc(x_loaded, 16)

                    with sp.Fori(0, BATCH // 2 - 1) as i:
                        load(2 * i + 2, 0)
                        store(2 * i, 0, i)
                        load(2 * i + 3, 1)
                        store(2 * i + 1, 1, i)
                    sp.wait_ge(ht_stored, 16 * (BATCH - 2))
                    sp.dma_start(ht_raw[:], HT_d[0]).then_inc(htr_loaded, 16)
                    store(BATCH - 2, 0, NG - 1)
                    store(BATCH - 1, 1, NG - 1)
                    sp.wait_ge(xl_ready, BATCH)
                    sp.wait_ge(h_stored, 16 * BATCH)
                    sp.wait_ge(ht_stored, 16 * BATCH)

                    def residual(j, par):
                        sp.dma_start(xres[par], x_rows[j]).then_inc(x_res, 16)

                    residual(0, 0)

                    def group(n, first, last):
                        for i in range(4):
                            j, par = 4 * n + i, i % 2
                            if not (last and i == 3):
                                sp.wait_ge(x_res, 16 * (j + 1))
                                if not (first and i == 0):
                                    sp.wait_ge(y_done, j)
                                    hold(sp, "sp")
                                residual(j + 1, 1 - par)
                            if i == 0 and not last:
                                sp.wait_ge(htl_ready, n + 1)
                                sp.dma_start(ht_raw[:], HT_d[n + 1]).then_inc(htr_loaded, 16)
                            sp.wait_ge(y_done, j + 1)
                            hold(sp, "sp")
                            if not (first and i == 0):
                                sp.wait_ge(y_stored, 16 * j)
                            sp.dma_start(out_rows[j], y[par]).then_inc(y_stored, 16)
                            if last and i < 3:
                                load_expert(sp, 1, 1, [i])

                    group(0, True, False)
                    sp.wait_ge(tab_ready, 1)
                    sp.dma_start(tab_d.rearrange("(b p) f -> p b f", p=P), tabi[:]).then_inc(tab_stored, 16)
                    sp.wait_ge(tab_stored, 16)
                    sp.dma_start(tab[:], tab_d.rearrange("(a n) f -> a (n f)", a=1)).then_inc(tab_loaded, 16)
                    with sp.Fori(1, NG - 1) as n:
                        group(n, False, False)
                    for par in range(2):
                        sp.wait_ge(scattered[par], 16 * 2 * TOPK * (BATCH // 2))
                    sp.dma_start(slot_s.rearrange("q c p a -> q c (p a)"),
                                 slot_d.rearrange("(c q p) a -> q c (p a)", q=P, p=P)).then_inc(slot_loaded, 16)
                    load_expert(sp, 0, 0)
                    group(NG - 1, False, True)
                    sp.wait_ge(tab_loaded, 16)
                    sp.wait_ge(pad_stored, 32)

                @block.gpsimd
                def _(pool):
                    def load_shared(n):
                        _, _, dst, src = shared_pieces[n]
                        pool.dma_start(dst, src).then_inc(shared_loaded, 16)

                    pool.wait_ge(cst_ready, 1)
                    load_shared(0)
                    for n, (hi, lo, piece, _) in enumerate(shared_pieces):
                        pool.wait_ge(shared_loaded, 16 * (n + 1))
                        if n + 1 < len(shared_pieces):
                            if n >= 1:
                                pool.wait_ge(sh_lo, n)
                            load_shared(n + 1)
                        pool.tensor_copy(hi, piece).then_inc(sh_hi, 1)
                        pool.wait_ge(sh_hi, n + 1)
                        pool.tensor_tensor(lo, piece, hi, ALU.subtract).then_inc(sh_lo, 1)

                    pool.wait_ge(slot_padded, 16 * (NCOL // P))

                    def scatter(b, par, turn):
                        pool.wait_ge(scat_ready, b + 1)
                        if turn is not None:
                            pool.wait_ge(scattered[par], 16 * 2 * TOPK * turn)
                        pool.tensor_copy(scI_now[par][:], scI[:, bass.ds(b * 2 * TOPK, 2 * TOPK)]).then_inc(picked, 1)
                        pool.tensor_copy(pair_now[par][:], pair[:, bass.ds(b * 2, 2), :, :]).then_inc(picked, 1)
                        pool.wait_ge(picked, 2 * b + 2)
                        hold(pool, "pool")
                        for i in range(2):
                            for k in range(TOPK):
                                n = i * TOPK + k
                                pool.indirect_dma_start(
                                    out=slot_d, out_offset=bass.IndirectOffsetOnAxis(ap=scI_now[par][:, n:n + 1], axis=0),
                                    in_=pair_now[par][:, i, k, :], in_offset=None,
                                    bounds_check=E * CAP - 1, oob_is_err=False).then_inc(scattered[par], 16)

                    for par in range(2):
                        scatter(par, par, None)
                    with pool.Fori(1, BATCH // 2) as i:
                        for par in range(2):
                            scatter(2 * i + par, par, i)
                    pool.wait_ge(h_stored, 16 * BATCH)
                    pool.wait_ge(pad_stored, 32)
                    pool.wait_ge(idxT_ready, 1)
                    pool.tensor_copy(idxc[:], idxT[:, 0:1]).then_inc(idx_ready, 1)
                    pool.wait_ge(idx_ready, 1)
                    hold(pool, "pool")
                    pool.indirect_dma_start(out=xg[:], out_offset=None, in_=H_d,
                                            in_offset=bass.IndirectOffsetOnAxis(ap=idxc[:], axis=0)).then_inc(xg_loaded, 16)

                @block.scalar
                def _(act):
                    act.wait_ge(at_loaded, 16)
                    act.copy(ath[:], at_raw[:]).then_inc(w_hi, 1)
                    act.wait_ge(x_loaded, 16)
                    act.copy(xh[0][:], xraw[0][:]).then_inc(xh_ready, 1)
                    act.wait_ge(wt_loaded, 16)
                    for k in range(KD):
                        act.copy(wth[:, k, :], wt_raw[:, k, :]).then_inc(w_hi, 1)
                    act.wait_ge(cst_loaded, 16 * 6)
                    act.copy(bth[:], bt_raw[:]).then_inc(w_hi, 1)
                    act.wait_ge(cst_ready, 1)

                    def split_x(b, par):
                        act.wait_ge(x_loaded, 16 * (b + 1))
                        act.copy(xh[par][:], xraw[par][:]).then_inc(xh_ready, 1)

                    def adapters(b):
                        act.wait_ge(xa_done, b + 1)
                        act.activation(xam[:], xa_ps[:, 0:SEQ], ACT.Copy, scale=amask[:, bass.ds(b, 1)]).then_inc(xam_ready, 1)
                        act.wait_ge(xam_ready, b + 1)
                        act.copy(xah[:], xam[:]).then_inc(xah_ready, 1)

                    split_x(1, 1)
                    adapters(0)

                    def slot(b, par, first, left):
                        for i in range(2):
                            act.wait_ge(h_done, 2 * b + i + 1)
                            if not first and i == 0:
                                act.wait_ge(h_stored, 16 * b)
                            act.copy(H_s[:, i, :], H_ps[i][:]).then_inc(h_copied, 1)
                        for i in range(2):
                            act.wait_ge(ht_done, 2 * b + i + 1)
                            if not first and i == 0:
                                act.wait_ge(ht_stored, 16 * b)
                            act.copy(HT_s[:, :, i * P:(i + 1) * P],
                                     HT_ps[i][:].rearrange("p (k t) -> p k t", k=KD)).then_inc(ht_copied, 1)
                        if left == 0:
                            columns_hi(0, True)
                        if left >= 1:
                            adapters(b + 1)
                        if left >= 2:
                            split_x(b + 2, par)
                        act.wait_ge(nm_ready, b + 1)
                        for i in range(2):
                            act.activation(ex[:, i, :], lg[:, i, :], ACT.Exp, bias=nm[:, i:i + 1],
                                           accum_out=S[:, i:i + 1]).then_inc(exp_done, 1)

                    def columns_hi(n, first):
                        act.wait_ge(htr_loaded, 16 * (n + 1))
                        if not first:
                            act.wait_ge(sgu_done, 6 * n)
                        act.copy(hth[:], ht_raw[:]).then_inc(hth_ready, 1)

                    def group(n, first, last):
                        for f, (f0, fw) in enumerate(FSC):
                            act.wait_ge(sgu_done, 6 * n + f + 1)
                            if f >= 2 or not first:
                                act.wait_ge(sm_ready, 6 * n + f - 1)
                            act.activation(sg[f % 2][0:fw, :], sg_ps[f % 2][0:fw, :], ACT.Silu).then_inc(ssilu_done, 1)
                            if f == 0 and not first:
                                act.wait_ge(so_done, 4 * n)
                            act.wait_ge(sm_ready, 6 * n + f + 1)
                            act.copy(smh[0:fw, f, :], sm[f % 2][0:fw, :]).then_inc(smh_ready, 1)
                        if last:
                            for q in range(NCH):
                                act.wait_ge(w_loaded, 16 * (q * NLD // NCH + 1))
                                act.copy(wh16[:, q, :], raw16[:, q, :]).then_inc(wh_ready, 1)
                        else:
                            columns_hi(n + 1, False)

                    over_batches(act, slot)
                    act.wait_ge(h_stored, 16 * BATCH)
                    over_groups(act, group)

                @block.vector
                def _(dve):
                    dve.memset(zero[:], 0.0).then_inc(zero_ready, 1)
                    dve.wait_ge(w_hi, 1)
                    dve.tensor_tensor(atl[:], at_raw[:], ath[:], ALU.subtract).then_inc(w_lo, 1)

                    def split_x(b, par):
                        dve.wait_ge(xh_ready, b + 1)
                        dve.tensor_tensor(xl[par][:], xraw[par][:], xh[par][:], ALU.subtract).then_inc(xl_ready, 1)

                    split_x(0, 0)
                    for k in range(KD):
                        dve.wait_ge(w_hi, k + 2)
                        dve.tensor_tensor(wtl[:, k, :], wt_raw[:, k, :], wth[:, k, :], ALU.subtract).then_inc(w_lo, 1)
                    dve.wait_ge(cst_loaded, 16 * 6)
                    pre = Steps(dve, "setup_step")
                    dve.tensor_copy(tri[:], c[:, C_TRI:C_TRI + P])
                    dve.tensor_copy(one[:], c[:, C_ONE:C_ONE + P])
                    dve.memset(acc[0][:, 0, :], 0.0)
                    pre.next(dve.tensor_copy(idf[:], idb[:]))
                    dve.tensor_scalar(amask[:], idf[:], c[:, C_AD:C_AD + 1], scl[:], ALU.is_equal, ALU.mult)
                    for par in range(2):
                        for i in range(2):
                            pre.next(dve.tensor_scalar(tokf[par][:, i:i + 1], c[:, C_P:C_P + 1],
                                                       float((2 * par + i - 4) * P), None, ALU.add))
                    dve.sem_inc(cst_ready, 1)
                    dve.wait_ge(w_hi, KD + 2)
                    dve.tensor_tensor(btl[:], bt_raw[:], bth[:], ALU.subtract).then_inc(w_lo, 1)

                    def adapters(b):
                        dve.wait_ge(xah_ready, b + 1)
                        dve.tensor_tensor(xal[:], xam[:], xah[:], ALU.subtract).then_inc(xal_ready, 1)

                    adapters(0)
                    split_x(1, 1)
                    st = Steps(dve, "routing_step")
                    NPLACE, NROUTE = 7, 13

                    def place(b, par, base):
                        st.n = 0
                        dve.wait_ge(pos_done, b + 1)
                        st.next(dve.tensor_tensor(prod[:], hot[par][:], pos.unsqueeze(2).to_broadcast([P, 2, TOPK, E]), ALU.mult), base)
                        st.next(dve.tensor_reduce(pos6[:], prod[:], AX.X, ALU.add), base)
                        st.next(dve.scalar_tensor_tensor(dst6[:], pos6[:], float(CAP - 1), base6[par][:], ALU.min, ALU.add), base)
                        st.next(dve.tensor_scalar(over[:], pos6[:], float(CAP), DROP, ALU.is_ge, ALU.mult), base)
                        st.next(dve.tensor_tensor(sc6[:], over[:], dst6[:], ALU.add), base)

                    def publish(b, par, base):
                        st.next(dve.tensor_scalar(tokf[par][:], tokf[par][:], float(4 * P), None, ALU.add), base)
                        to = pair[:, bass.ds(b * 2, 2), :, :]
                        dve.tensor_copy(to[:, :, :, 0], tokf[par][:].unsqueeze(2).to_broadcast([P, 2, TOPK]))
                        dve.tensor_copy(to[:, :, :, 1], w6[par][:])
                        st.next(dve.tensor_copy(scI[:, bass.ds(b * 2 * TOPK, 2 * TOPK)], sc6[:].rearrange("p i k -> p (i k)")), base)
                        dve.sem_inc(scat_ready, 1)

                    def route(b, par, base, left):
                        dve.wait_ge(lg_done, b + 1)
                        dve.tensor_reduce(nm[:], lg, AX.X, ALU.max, negate=True).then_inc(nm_ready, 1)
                        if left >= 2:
                            split_x(b + 2, par)
                        dve.wait_ge(exp_done, 2 * b + 2)
                        st.next(dve.reciprocal(rS[:], S[:]), base)
                        st.next(dve.tensor_tensor(sc[:], ex[:], rS[:].unsqueeze(2).to_broadcast([P, 2, E]), ALU.mult), base)
                        for i in range(2):
                            hold(dve, "dve")
                            st.next(dve.max(top8[:, i, :], sc[:, i, :]), base)
                            hold(dve, "dve")
                            st.next(dve.max_index(ix8[:, i, :], top8[:, i, :], sc[:, i, :]), base)
                        st.next(dve.tensor_copy(ixf[:], ix8[:, :, 0:TOPK]), base)
                        st.next(dve.tensor_reduce(ssum[:], top8[:, :, 0:TOPK], AX.X, ALU.add), base)
                        st.next(dve.tensor_scalar(ssum[:], ssum[:], 1e-20, None, ALU.add), base)
                        st.next(dve.reciprocal(rsum[:], ssum[:]), base)
                        dve.tensor_tensor(w6[par][:], top8[:, :, 0:TOPK], rsum[:].unsqueeze(2).to_broadcast([P, 2, TOPK]), ALU.mult)
                        dve.tensor_scalar(base6[par][:], ixf[:], float(CAP), None, ALU.mult)
                        st.next(dve.tensor_tensor(
                            hot[par][:], c[:, C_IOTA:C_IOTA + E].unsqueeze(1).unsqueeze(1).to_broadcast([P, 2, TOPK, E]),
                            ixf[:].unsqueeze(3).to_broadcast([P, 2, TOPK, E]), ALU.is_equal), base)
                        with nc.allow_low_precision(reason="sums of whole numbers up to 32"):
                            st.next(dve.tensor_reduce(M[par][:], hot[par][:].rearrange("p i k e -> p i e k"), AX.X, ALU.add), base)
                            st.next(dve.tensor_tensor(acc[par][:, 1, :], acc[par][:, 0, :], M[par][:, 0, :], ALU.add), base)
                            dve.tensor_tensor(acc[1 - par][:, 0, :], acc[par][:, 1, :], M[par][:, 1, :],
                                              ALU.add).then_inc(m_ready, 1)

                    NST = NPLACE + NROUTE

                    def columns_lo(n):
                        dve.wait_ge(hth_ready, n + 1)
                        dve.tensor_tensor(htl[:], ht_raw[:], hth[:], ALU.subtract).then_inc(htl_ready, 1)

                    def slot(b, par, first, left):
                        base = 0 if first else NST * b - NPLACE
                        st.n = 0
                        if not first:
                            place(b - 1, 1 - par, base)
                            publish(b - 1, 1 - par, base)
                        if left == 0:
                            columns_lo(0)
                        else:
                            adapters(b + 1)
                        route(b, par, base, left)
                        assert st.n == (NROUTE if first else NST)

                    over_batches(dve, slot)

                    def combine(n, i, first):
                        j, par = 4 * n + i, i % 2
                        dve.wait_ge(so_done, j + 1)
                        dve.wait_ge(x_res, 16 * (j + 1))
                        if not (first and i < 2):
                            dve.wait_ge(y_stored, 16 * (j - 1))
                        dve.tensor_tensor(y[par], so_ps[par][:], xres[par], ALU.add).then_inc(y_done, 1)

                    def hidden(n, f, fw):
                        up = su_ps[f % 2][:]
                        if f == 5:
                            dve.wait_ge(sgu_done, 6 * n + f + 1)
                            dve.tensor_copy(up5[0:HALF, :], sg_ps[1][HALF:P, :]).then_inc(up_moved, 1)
                            dve.wait_ge(up_moved, n + 1)
                            up = up5[0:HALF, :]
                        dve.wait_ge(ssilu_done, 6 * n + f + 1)
                        dve.tensor_tensor(sm[f % 2][0:fw, :], sg[f % 2][0:fw, :], up, ALU.mult).then_inc(sm_ready, 1)
                        dve.wait_ge(smh_ready, 6 * n + f + 1)
                        low = sml[:, f, :] if f < 5 else smh[HALF:P, f, :]
                        dve.tensor_tensor(low, sm[f % 2][0:fw, :], smh[0:fw, f, :], ALU.subtract).then_inc(sml_ready, 1)

                    def group(n, first, last):
                        for f, (f0, fw) in enumerate(FSC):
                            hidden(n, f, fw)
                            if first and f == 1:
                                base = NST * BATCH - NPLACE
                                place(BATCH - 1, 1, base)
                                publish(BATCH - 1, 1, base)
                                count_tiles()
                        if first:
                            own_tiles()
                        if last:
                            dve.wait_ge(slotT_done, 1)
                            dve.tensor_copy(wT[:], lg_ps[:])
                            dve.tensor_copy(idxT[:], misc_ps[:]).then_inc(idxT_ready, 1)
                        else:
                            columns_lo(n + 1)
                        for i in range(4):
                            if last:
                                for q in range(2 * i, 2 * i + 2):
                                    dve.wait_ge(wh_ready, q + 1)
                                    dve.tensor_tensor(wl16[:, q, :], raw16[:, q, :], wh16[:, q, :],
                                                      ALU.subtract).then_inc(wl_ready, 1)
                            combine(n, i, first)
                        if first:
                            tile_table()

                    tb = Steps(dve, "table_step")

                    def count_tiles():
                        dve.wait_ge(cnt_done, 1)
                        tb.next(dve.tensor_copy(cntE[:], misc_ps[0:E, 0:1]))
                        for j in range(1, CT):
                            dve.tensor_scalar(gtj[:, j - 1:j], cntE[:], float(j * P), None, ALU.is_gt).then_inc(tb.sem, 1)
                            tb.n += 1
                        dve.wait_ge(tb.sem, tb.n)
                        tb.next(dve.tensor_reduce(eT[:, 0:1], gtj[:], AX.X, ALU.add))
                        tb.next(dve.tensor_scalar(eT[:, 0:1], eT[:, 0:1], 1.0, None, ALU.add))
                        dve.sem_inc(tiles_ready, 1)

                    def own_tiles():
                        dve.wait_ge(first_done, 1)
                        dve.tensor_copy(eT[:, 1:2], misc_ps[0:E, 1:2])
                        dve.tensor_copy(tot[:, 0:1], misc_ps[0:1, 2:3])
                        dve.tensor_scalar(tot[:, 1:2], misc_ps[0:1, 2:3], -3.0, None, ALU.add)
                        tb.next(dve.tensor_copy(eT[:, 2:3], c[0:E, C_E:C_E + 1]))
                        tb.next(dve.tensor_tensor(gend[:], eT[:, 0:1], eT[:, 1:2], ALU.add))
                        dve.tensor_scalar(m1[:], c[0:E, C_G:C_G + NCOL], gend[:], None, ALU.is_ge)
                        tb.next(dve.tensor_scalar(m2[:], c[0:E, C_G:C_G + NCOL], eT[:, 1:2], None, ALU.is_ge))
                        dve.tensor_tensor(m2[:], m2[:], m1[:], ALU.subtract).then_inc(hot_ready, 1)

                    def tile_table():
                        dve.wait_ge(tg_done, 1)
                        tb.next(dve.tensor_copy(tg[:], misc_ps[:, 16:28].rearrange("p (b f) -> p b f", b=4)))
                        tb.next(dve.tensor_copy(bnd[:], misc_ps[0:1, 64:64 + E]))
                        T_, G_, E_ = tg[:, :, 0], tg[:, :, 1], tg[:, :, 2]
                        tb.next(dve.tensor_tensor(tt[:], c[:, C_TG:C_TG + 4], G_, ALU.subtract))
                        dve.tensor_scalar(t8[:], tt[:], float(NCH), None, ALU.mult)
                        tb.next(dve.tensor_scalar(t8b[:], tt[:], float(NCH), float(NCH), ALU.mult, ALU.add))
                        tb.next(dve.tensor_tensor(mT[:], c[:, C_M:C_M + NCH].unsqueeze(1).to_broadcast([P, 4, NCH]),
                                                  T_.unsqueeze(2).to_broadcast([P, 4, NCH]), ALU.mult))
                        for f, t in ((0, t8), (1, t8b)):
                            tb.next(dve.tensor_tensor(cmp_[:], t[:].unsqueeze(2).to_broadcast([P, 4, NCH]), mT[:], ALU.is_ge))
                            tb.next(dve.tensor_reduce(fq[:], cmp_[:], AX.X, ALU.add))
                            tb.next(dve.scalar_tensor_tensor(qf[f][:], E_, float(NCH), fq[:], ALU.mult, ALU.add))
                            tb.next(dve.tensor_scalar(qf[f][:], qf[f][:], float(NCH), None, ALU.add))
                        dve.tensor_scalar(qf[2][:], T_, 1.0, None, ALU.is_equal)
                        tb.next(dve.scalar_tensor_tensor(qf[3][:], E_, float(CT), tt[:], ALU.mult, ALU.add))
                        for f in range(3):
                            dve.tensor_copy(qi[f][:], qf[f][:]).then_inc(tb.sem, 1)
                        tb.n += 3
                        tb.next(dve.tensor_copy(tabi[:, :, T_COL], qf[3][:]))
                        dve.tensor_single_scalar(qs[0][:], qi[1][:], 10, ALU.logical_shift_left)
                        tb.next(dve.tensor_single_scalar(qs[1][:], qi[2][:], 20, ALU.logical_shift_left))
                        tb.next(dve.tensor_tensor(qs[2][:], qs[0][:], qs[1][:], ALU.bitwise_or))
                        dve.tensor_tensor(tabi[:, :, T_WORD], qs[2][:], qi[0][:], ALU.bitwise_or).then_inc(tab_ready, 1)

                    dve.wait_ge(ht_stored, 16 * BATCH)
                    over_groups(dve, group)
                    dve.wait_ge(idxT_ready, 1)

                @block.tensor
                def _(pe):
                    def place(b, par):
                        pe.wait_ge(m_ready, b + 1)
                        for i in range(2):
                            nc.tensor.matmul(pos[:, i, :], tri[:], M[par][:, i, :], start=True, stop=False)
                            last = nc.tensor.matmul(pos[:, i, :], one[:], acc[par][:, i, :], start=False, stop=True)
                        last.then_inc(pos_done, 1)

                    def adapters(b, par):
                        pe.wait_ge(xh_ready, b + 1)
                        pe.wait_ge(xl_ready, b + 1)
                        for k in range(KD):
                            last = split_mm(xa_ps[:, 0:SEQ], ath[:, k, :], atl[:, k, :], xh[par][:, k, :], xl[par][:, k, :],
                                            k == 0, k == KD - 1)
                        last.then_inc(xa_done, 1)

                    pe.wait_ge(w_lo, 1)
                    adapters(0, 0)

                    def slot(b, par, first, left):
                        for i in range(2):
                            for k in range(KD):
                                if first and i == 0:
                                    pe.wait_ge(w_lo, k + 2)
                                split_mm(H_ps[i][:], xh[par][:, k, i * P:(i + 1) * P], xl[par][:, k, i * P:(i + 1) * P],
                                         wth[:, k, :], wtl[:, k, :], k == 0, False)
                        if first:
                            pe.wait_ge(w_lo, KD + 2)
                        pe.wait_ge(xal_ready, b + 1)
                        for i in range(2):
                            split_mm(H_ps[i][:], xah[:, i * P:(i + 1) * P], xal[:, i * P:(i + 1) * P], bth[:], btl[:],
                                     False, True).then_inc(h_done, 1)
                        for i in range(2):
                            pe.wait_ge(h_copied, 2 * b + i + 1)
                            for k in range(KD):
                                last = nc.tensor.transpose(HT_ps[i][:, k * P:(k + 1) * P], H_s[:, i, k * P:(k + 1) * P], ident[:])
                            last.then_inc(ht_done, 1)
                        if not first:
                            place(b - 1, 1 - par)
                        if left >= 1:
                            adapters(b + 1, 1 - par)
                        for i in range(2):
                            pe.wait_ge(ht_copied, 2 * b + i + 1)
                            for k in range(KD):
                                last = nc.tensor.matmul(lg[:, i, :], HT_s[:, k, i * P:(i + 1) * P], gw[:, k, :],
                                                        start=(k == 0), stop=(k == KD - 1))
                        last.then_inc(lg_done, 1)

                    def group(n, first, last_):
                        pe.wait_ge(hth_ready, n + 1)
                        pe.wait_ge(htl_ready, n + 1)
                        for f, (f0, fw) in enumerate(FSC):
                            if first and f == 2:
                                place(BATCH - 1, 1)
                                nc.tensor.matmul(misc_ps[0:E, 0:1], acc[0][:, 0, :], one[:, 0:1],
                                                 start=True, stop=True).then_inc(cnt_done, 1)
                            if f >= 2 or not first:
                                pe.wait_ge(sm_ready, 6 * n + f - 1)
                            for a, dst in ((f0, sg_ps[f % 2]), (FS5 + f0, su_ps[f % 2])) if f < 5 else ((2 * FS5, sg_ps[1]),):
                                for k in range(KD):
                                    last = split_mm(dst[:], shgh[:, k, a:a + P], shgl[:, k, a:a + P],
                                                    hth[:, k, :], htl[:, k, :], k == 0, k == KD - 1)
                            last.then_inc(sgu_done, 1)
                        if first:
                            pe.wait_ge(tiles_ready, 1)
                            nc.tensor.matmul(misc_ps[0:E, 1:2], c[0:E, C_TRI:C_TRI + E], eT[:, 0:1], start=True, stop=True)
                            nc.tensor.matmul(misc_ps[0:1, 2:3], c[0:E, C_ONE:C_ONE + 1], eT[:, 0:1],
                                             start=True, stop=True).then_inc(first_done, 1)
                            pe.wait_ge(scat_ready, BATCH)
                        if last_:
                            pe.wait_ge(slot_loaded, 16)
                            pe.wait_ge(tab_ready, 1)
                            for m in range(4):
                                nc.tensor.transpose(misc_ps[:, m * P:(m + 1) * P], slot_s[:, m, :, 0], ident[:])
                                last = nc.tensor.transpose(lg_ps[:, m * P:(m + 1) * P], slot_s[:, m, :, 1], ident[:])
                            last.then_inc(slotT_done, 1)
                        for i in range(4):
                            if not (first and i < 2):
                                pe.wait_ge(y_done, 4 * n + i - 1)
                            for f, (f0, fw) in enumerate(FSC):
                                if i == 0:
                                    pe.wait_ge(sml_ready, 6 * n + f + 1)
                                t = slice(i * P, (i + 1) * P)
                                if f < 5:
                                    split_mm(so_ps[i % 2][:], smh[:, f, t], sml[:, f, t], shdh[:, f, :], shdl[:, f, :], f == 0, False)
                                else:
                                    nc.tensor.matmul(so_ps[i % 2][:], smh[:, f, t], shdh[:, f, :], start=False, stop=False)
                                    last = nc.tensor.matmul(so_ps[i % 2][:], smh[0:HALF, f, t], shdl[0:HALF, f, :],
                                                            start=False, stop=True)
                            last.then_inc(so_done, 1)
                        if first:
                            pe.wait_ge(hot_ready, 1)
                            for m in range(4):
                                nc.tensor.matmul(misc_ps[:, 16 + 3 * m:19 + 3 * m], m2[:, m * P:(m + 1) * P], eT[:],
                                                 start=True, stop=True)
                            nc.tensor.matmul(misc_ps[0:1, 64:64 + E], gend[:], c[0:E, C_ID:C_ID + E],
                                             start=True, stop=True).then_inc(tg_done, 1)

                    over_batches(pe, slot)
                    pe.wait_ge(sh_lo, len(shared_pieces))
                    over_groups(pe, group)

        with ExitStack() as ctx:
            xgh, xgl = sb(ctx, "xgh", [P, D], f32r), sb(ctx, "xgl", [P, D], f32r)
            gs = sb(ctx, "gs", [P, F])
            hm = sb(ctx, "hm", [P, F])
            hh, hl = sb(ctx, "hh", [P, 3 * P], f32r), sb(ctx, "hl", [P, 3 * P], f32r)
            idxd = sb(ctx, "idxd", [P, 1], i32)
            eo = sb(ctx, "eo", [P, D])
            g_ps, u_ps, xt_ps, ht_ps, o_ps = (ps(ctx, n) for n in ("g_ps", "u_ps", "xt_ps", "ht_ps", "o_ps"))
            tx_done = sem("tx_done")
            xgh_ready, xgl_ready, gu_done, silu_done = sem("xgh_ready"), sem("xgl_ready"), sem("gu_done"), sem("silu_done")
            hm_ready, th_done, hh_ready, hl_ready = sem("hm_ready"), sem("th_done"), sem("hh_ready"), sem("hl_ready")
            d_done, eo_ready, idxd_ready, added = sem("d_done"), sem("eo_ready"), sem("idxd_ready"), sem("added")

            def field(eng, g, f, lo, hi):
                return eng.value_load(tab[0:1, bass.ds(g * NF + f, 1)], min_val=lo, max_val=hi)

            def tiles(eng):
                return eng.value_load(tot[0:1, 0:1], min_val=E, max_val=E * CT)

            def last_tile(eng):
                return eng.value_load(tot[0:1, 1:2], min_val=E - 3, max_val=E * CT - 3) + 2

            with nc.Block() as block:
                @block.sync
                def _(sp):
                    load_expert(sp, 1, 1, [3])
                    with sp.Fori(1, E // 2) as i:
                        for par in range(2):
                            sp.wait_ge(wl_ready, NCH * (2 * i + par - 1))
                            hold(sp, "sp")
                            load_expert(sp, 2 * i + par, par)
                    sp.wait_ge(w_loaded, 16 * NLD * E)
                    sp.sem_inc(w_loaded, 16 * NLD)

                @block.gpsimd
                def _(pool):
                    total = tiles(pool)

                    def gather(g):
                        col = field(pool, g, T_COL, 0, NCOL - 1)
                        pool.wait_ge(xg_loaded, 16 * g)
                        pool.wait_ge(tx_done, g)
                        pool.tensor_copy(idxc[:], idxT[:, bass.ds(col, 1)]).then_inc(idx_ready, 1)
                        pool.wait_ge(idx_ready, g + 1)
                        hold(pool, "pool")
                        pool.indirect_dma_start(out=xg[:], out_offset=None, in_=H_d,
                                                in_offset=bass.IndirectOffsetOnAxis(ap=idxc[:], axis=0)).then_inc(xg_loaded, 16)

                    def add_rows(g, first):
                        col = field(pool, g, T_COL, 0, NCOL - 1)
                        if not first:
                            pool.wait_ge(added, 16 * g)
                        pool.tensor_copy(idxd[:], idxT[:, bass.ds(col, 1)]).then_inc(idxd_ready, 1)
                        pool.wait_ge(idxd_ready, g + 1)
                        pool.wait_ge(eo_ready, g + 1)
                        hold(pool, "pool")
                        pool.indirect_dma_start(out=out, out_offset=bass.IndirectOffsetOnAxis(ap=idxd[:], axis=0),
                                                in_=eo[:], in_offset=None, compute_op=ALU.add).then_inc(added, 16)

                    for g in range(1, 4):
                        gather(g)
                    pool.wait_ge(y_stored, 16 * (TOK // P))
                    add_rows(0, True)
                    with pool.Fori(4, total + 1) as g:
                        gather(g)
                        add_rows(g - 3, False)
                    last = last_tile(pool)
                    for back in (1, 0):
                        add_rows(last - back, False)
                    pool.wait_ge(added, 16 * total)
                    hold(pool, "pool")

                @block.scalar
                def _(act):
                    total = tiles(act)

                    def rows_hi(g):
                        act.wait_ge(tx_done, g + 1)
                        act.copy(xgh[:], xt_ps[:]).then_inc(xgh_ready, 1)

                    rows_hi(0)

                    def split_weights(g, word, fresh):
                        qb = act.snap(word & 1023)
                        act.wait_ge(w_loaded, ((qb >> (NCH.bit_length() - 1)) + 1) * (16 * NLD))
                        if not fresh:
                            act.wait_ge(d_done, (word >> 20) + g)
                        with act.Fori(qb, (word >> 10) & 1023) as q:
                            act.copy(wh16[:, q % (2 * NCH), :], raw16[:, q % (2 * NCH), :]).then_inc(wh_ready, 1)

                    def slot(g, last=False):
                        act.wait_ge(gu_done, g + 1)
                        act.activation(gs[:], g_ps[:, 0:F], ACT.Silu).then_inc(silu_done, 1)
                        if not last:
                            rows_hi(g + 1)
                            word = field(act, g + 1, T_WORD, 0, (1 << 21) - 1)
                        act.wait_ge(th_done, g + 1)
                        act.copy(hh[:, 0:2 * P], ht_ps[:, 0:2 * P])
                        act.copy(hh[0:96, 2 * P:3 * P], ht_ps[0:96, 2 * P:3 * P]).then_inc(hh_ready, 1)
                        if not last:
                            split_weights(g + 1, word, False)

                    split_weights(0, field(act, 0, T_WORD, 0, (1 << 21) - 1), True)
                    slot(0)
                    with act.Fori(1, total - 1) as g:
                        slot(g)
                    slot(last_tile(act), True)

                @block.vector
                def _(dve):
                    total = tiles(dve)
                    dve.sem_inc(d_done, 1)

                    def rows_lo(g):
                        dve.wait_ge(xgh_ready, g + 1)
                        dve.tensor_tensor(xgl[:], xt_ps[:], xgh[:], ALU.subtract).then_inc(xgl_ready, 1)

                    rows_lo(0)

                    def weigh(g, second=False):
                        col = field(dve, g, T_COL, 0, NCOL - 1)
                        dve.wait_ge(d_done, g + 2)
                        if not second:
                            dve.wait_ge(added, 16 * g)
                        dve.tensor_scalar(eo[:], o_ps[:], wT[:, bass.ds(col, 1)], None, ALU.mult).then_inc(eo_ready, 1)

                    def split_weights(word):
                        with dve.Fori(word & 1023, (word >> 10) & 1023) as q:
                            dve.wait_ge(wh_ready, q + 1)
                            dve.tensor_tensor(wl16[:, q % (2 * NCH), :], raw16[:, q % (2 * NCH), :], wh16[:, q % (2 * NCH), :],
                                              ALU.subtract).then_inc(wl_ready, 1)

                    def slot(g, first=False, second=False, last=False):
                        dve.wait_ge(silu_done, g + 1)
                        dve.tensor_tensor(hm[:], gs[:], u_ps[:, 0:F], ALU.mult).then_inc(hm_ready, 1)
                        if not last:
                            rows_lo(g + 1)
                            word = field(dve, g + 1, T_WORD, 0, (1 << 21) - 1)
                        if not first:
                            weigh(g - 1, second)
                        dve.wait_ge(hh_ready, g + 1)
                        dve.tensor_tensor(hl[:, 0:2 * P], ht_ps[:, 0:2 * P], hh[:, 0:2 * P], ALU.subtract)
                        dve.tensor_tensor(hl[0:96, 2 * P:3 * P], ht_ps[0:96, 2 * P:3 * P], hh[0:96, 2 * P:3 * P],
                                          ALU.subtract).then_inc(hl_ready, 1)
                        if not last:
                            split_weights(word)

                    split_weights(field(dve, 0, T_WORD, 0, (1 << 21) - 1))
                    slot(0, first=True)
                    slot(1, second=True)
                    with dve.Fori(2, total - 1) as g:
                        slot(g)
                    last = last_tile(dve)
                    slot(last, last=True)
                    weigh(last)

                @block.tensor
                def _(pe):
                    total = tiles(pe)

                    def transpose_rows(g):
                        pe.wait_ge(xg_loaded, 16 * (g + 1))
                        for k in range(KD):
                            last = nc.tensor.transpose(xt_ps[:, k * P:(k + 1) * P], xg[:, k * P:(k + 1) * P], ident[:])
                        last.then_inc(tx_done, 1)

                    def down(g, par):
                        pe.wait_ge(hh_ready, g + 1)
                        pe.wait_ge(hl_ready, g + 1)
                        for n, (f0, fw) in enumerate(FC):
                            o = par * WROW + DN0 + n * D
                            last = split_mm(o_ps[:], hh[0:fw, f0:f0 + P], hl[0:fw, f0:f0 + P],
                                            wh[0:fw, o:o + D], wl[0:fw, o:o + D], n == 0, n == len(FC) - 1)
                        last.then_inc(d_done, 1)

                    def gate_up(g, par):
                        pe.wait_ge(xgh_ready, g + 1)
                        pe.wait_ge(xgl_ready, g + 1)
                        for k in range(KD):
                            for o, dst in ((0, g_ps), (F, u_ps)):
                                a = par * WROW + GU0 + k * 2 * F + o
                                last = split_mm(dst[:, 0:F], xgh[:, k * P:(k + 1) * P], xgl[:, k * P:(k + 1) * P],
                                                wh[:, a:a + F], wl[:, a:a + F], k == 0, k == KD - 1)
                        last.then_inc(gu_done, 1)

                    def transpose_h(g):
                        pe.wait_ge(hm_ready, g + 1)
                        for n, (f0, fw) in enumerate(FC):
                            last = nc.tensor.transpose(ht_ps[0:fw, n * P:(n + 1) * P], hm[:, f0:f0 + fw], ident[:])
                        last.then_inc(th_done, 1)

                    def expert(e, par, g0, first=False):
                        pe.wait_ge(wl_ready, NCH * (e + 1))
                        gate_up(g0, par)
                        end = pe.value_load(bnd[0:1, bass.ds(e, 1)], min_val=1, max_val=E * CT)
                        transpose_rows(g0 + 1)
                        if not first:
                            down(g0 - 1, 1 - par)
                        transpose_h(g0)
                        with pe.If(end > g0 + 1):
                            with pe.Fori(g0 + 1, end) as g:
                                gate_up(g, par)
                                transpose_rows(g + 1)
                                down(g - 1, par)
                                transpose_h(g)
                        return end

                    transpose_rows(0)
                    expert(1, 1, expert(0, 0, 0, True))
                    with pe.Fori(1, E // 2) as i:
                        g0 = pe.value_load(bnd[0:1, bass.ds(2 * i - 1, 1)], min_val=1, max_val=E * CT)
                        expert(2 * i + 1, 1, expert(2 * i, 0, g0))
                    down(last_tile(pe), 1)


def kernel(x, itok_B_0_6, L0_cond_W, L0_cond_A, L0_cond_Bm, L0_cond_scalings, L0_ffn_gate_w, L0_ffn_w_gate, L0_ffn_w_up,
           L0_ffn_w_down, L0_ffn_sh_gate, L0_ffn_sh_up, L0_ffn_sh_down):
    import numpy as np
    import concourse.bacc as bacc
    from concourse.bass_utils import run_bass_kernel_spmd as run

    def chunks(a):
        return a.T.reshape(KD, P, -1).transpose(1, 0, 2)

    cst = np.zeros((P, NCONST), np.float32)
    cst[:, C_ID:C_ID + P] = np.eye(P)
    cst[:, C_TRI:C_TRI + P] = np.triu(np.ones((P, P)), 1)
    cst[:, C_ONE:C_ONE + P] = 1
    cst[:, C_IOTA:C_IOTA + E] = np.arange(E)
    cst[:, C_G:C_G + NCOL] = np.arange(NCOL)
    cst[:, C_TG:C_TG + 4] = np.arange(4)[None] * P + np.arange(P)[:, None]
    cst[:, C_M:C_M + NCH] = np.arange(1, NCH + 1)
    cst[:, C_AD] = np.arange(P) // 16
    cst[:, C_P] = np.arange(P)
    cst[:, C_E] = np.arange(P)

    wgu = np.concatenate([L0_ffn_w_gate, L0_ffn_w_up], 1)
    wgu = wgu.transpose(0, 2, 1).reshape(E, KD, P, 2 * F).transpose(0, 2, 1, 3).reshape(E, P, KD * 2 * F)
    wdn = np.zeros((E, 3 * P, D), np.float32)
    wdn[:, :F] = L0_ffn_w_down.transpose(0, 2, 1)
    wdn = wdn.reshape(E, 3, P, D).transpose(0, 2, 1, 3).reshape(E, P, 3 * D)
    dn = L0_ffn_sh_down.T
    arrays = {
        "xT": x.transpose(0, 2, 1).reshape(BATCH, KD, P, SEQ).transpose(0, 2, 1, 3),
        "xn": x.reshape(TOK, D),
        "WT": chunks(L0_cond_W),
        "AT": chunks(L0_cond_A.reshape(P, D)),
        "BT": L0_cond_Bm.transpose(0, 2, 1).reshape(P, D),
        "scal": np.repeat(L0_cond_scalings, 16).reshape(P, 1),
        "idx": np.broadcast_to(itok_B_0_6.reshape(1, BATCH), (P, BATCH)),
        "gwT": chunks(L0_ffn_gate_w),
        "cst": cst,
        "pad": np.broadcast_to(np.stack([np.arange(TOK, TOK + P), np.zeros(P)], 1).astype(np.float32).reshape(1, 2 * P), (P, 2 * P)),
        "shg": chunks(np.concatenate([L0_ffn_sh_gate[:FS5], L0_ffn_sh_up[:FS5], L0_ffn_sh_gate[FS5:], L0_ffn_sh_up[FS5:]], 0)).reshape(P, -1),
        "shd": np.concatenate([dn, dn[FS5:]], 0).reshape(6, P, D).transpose(1, 0, 2),
        "wE": np.concatenate([wgu, wdn], 2),
    }
    arrays = {f"{k}_dram": np.ascontiguousarray(v) for k, v in arrays.items()}
    nc = bacc.Bacc("TRN2", target_bir_lowering=False, num_devices=1)
    args = [nc.dram_tensor(k, v.shape, mybir.dt.from_np(v.dtype), kind="ExternalInput").ap() for k, v in arrays.items()]
    out = nc.dram_tensor("out_dram", (TOK + P, D), mybir.dt.float32, kind="ExternalOutput").ap()
    moe_kernel(nc, *args, out)
    r = run(nc, [arrays], core_ids=[0])
    return r.results[0]["out_dram"][:TOK].reshape(BATCH, SEQ, D)
```
